# Optimizing a Trainium2 kernel written in Bass

```python
import numpy as np
import jax
import jax.numpy as jnp

def _softmax(x, axis=-1):
    return jax.nn.softmax(x, axis=axis)

def _gelu(x):
    return jax.nn.gelu(x, approximate=True)

def _silu(x):
    return jax.nn.silu(x)

def _sigmoid(x):
    return jax.nn.sigmoid(x)

def _layernorm(x, axis=-1, eps=1e-05):
    m = jnp.mean(x, axis=axis, keepdims=True)
    v = jnp.var(x, axis=axis, keepdims=True)
    return (x - m) / jnp.sqrt(v + eps)

def _scatter_add(tgt, idx, src, axis=0):
    return tgt.at[idx].add(src)

def _segment_sum(src, seg, n):
    return jax.ops.segment_sum(src, seg, n)
kernel_name = 'mk_flamingo_gated_d2_seqx_r8_6703db'

def setup_inputs(seed: int=0):
    np.random.seed(seed)
    _w = jnp.asarray

    def _rec_inputs():
        import jax
        import jax.numpy as jnp
        _rk = jax.random.key(seed)
        x = -0.0002928 + 1 * jax.random.normal(jax.random.fold_in(_rk, 1), (32, 128, 128), jnp.float32)
        _lenS = 128 - jax.random.randint(jax.random.fold_in(_rk, 7), (32,), 0, max(1, 128 // 4) + 1, jnp.int32)
        _lenS2 = 120 - jax.random.randint(jax.random.fold_in(_rk, 8), (32,), 0, max(1, 120 // 4) + 1, jnp.int32)
        _ctx_1024P = jax.random.normal(jax.random.fold_in(_rk, 11), (32, 16, 128), jnp.float32)
        _ctx_1024c = jax.random.dirichlet(jax.random.fold_in(_rk, 511), 0.3 * jnp.ones((16,), jnp.float32), (32, 120))
        _ctx_1024t = jnp.einsum('bsk,bkd->bsd', _ctx_1024c, _ctx_1024P)
        _ctx_1024t = _ctx_1024t * jax.lax.rsqrt(jnp.mean(jnp.square(_ctx_1024t)) + 1e-12) * 0.953939
        ctx_1024 = -1.39393e-06 + 0.999914 * (_ctx_1024t + 0.3 * jax.random.normal(jax.random.fold_in(_rk, 611), (32, 120, 128), jnp.float32))
        fside_BxSxS2_0 = -1.47943e-05 + 1.00017 * jax.random.normal(jax.random.fold_in(_rk, 13), (32, 128, 120), jnp.float32)
        _validS = jnp.arange(128)[None, :] < _lenS[:, None]
        _validS2 = jnp.arange(120)[None, :] < _lenS2[:, None]
        _causal = jnp.tril(jnp.ones((128, 128), dtype=bool))
        mask_1x1xSxS2_bk0 = jnp.logical_not(jnp.broadcast_to(_validS2[0:1, None, None, :], (1, 1, 128, 120)))
        mask_BxS2_bf0 = jnp.logical_not(jnp.ones((32, 120), dtype=bool))
        _g = jax.random.normal(jax.random.fold_in(_rk, 9001), (2, 2), jnp.float32)
        _g = jnp.sign(_g) * jnp.maximum(jnp.abs(_g), 1.0) + (_g == 0) * 1.0
        g_xattn = _g[0]
        g_ffn = _g[1]
        return (x, ctx_1024, fside_BxSxS2_0, mask_1x1xSxS2_bk0, mask_BxS2_bf0, g_xattn, g_ffn)
    x, ctx_1024, fside_BxSxS2_0, mask_1x1xSxS2_bk0, mask_BxS2_bf0, g_xattn, g_ffn = _rec_inputs()

    def _L0_xattn_setup():
        import jax, jax.numpy as jnp
        import numpy as np
        D_MODEL = 128
        H = 16
        DK = D_MODEL // H
        B, S = (2, 256)
        NEG = -1000000000.0
        key = jax.random.key(seed)
        ks = jax.random.split(key, 7)
        scale = 1.0 / np.sqrt(D_MODEL)
        inp = {'q': jax.random.normal(ks[0], (B, S, D_MODEL), jnp.float32), 'k': jax.random.normal(ks[1], (B, S, D_MODEL), jnp.float32), 'v': jax.random.normal(ks[2], (B, S, D_MODEL), jnp.float32), 'mask': jnp.tril(jnp.ones((S, S), dtype=bool))[None, None, :, :], 'w_q': jax.random.normal(ks[3], (D_MODEL, D_MODEL), jnp.float32) * scale, 'w_k': jax.random.normal(ks[4], (D_MODEL, D_MODEL), jnp.float32) * scale, 'w_v': jax.random.normal(ks[5], (D_MODEL, D_MODEL), jnp.float32) * scale, 'w_o': jax.random.normal(ks[6], (D_MODEL, D_MODEL), jnp.float32) * scale}
        return inp
    _L0_xattn_all = _L0_xattn_setup()
    _L0_xattn_in = {k: v for k, v in _L0_xattn_all.items() if k in ('w_q', 'w_k', 'w_v', 'w_o')}
    del _L0_xattn_all

    def _L0_ffn_setup():
        import jax, jax.numpy as jnp
        import numpy as np
        E = 64
        K = 6
        CAP = 64
        ROUTE_SCALE = 1.0
        key = jax.random.key(seed)
        ks = jax.random.split(key, 9)
        B, S, D, I = (2, 128, 128, 88)
        SI = 2 * I
        s = 0.02
        return {'x': jax.random.normal(ks[0], (B, S, D), jnp.float32), 'gate_w': jax.random.normal(ks[1], (E, D), jnp.float32) * s, 'gate_b': jnp.zeros((E,), jnp.float32), 'w1': jax.random.normal(ks[2], (E, I, D), jnp.float32) * s, 'w2': jax.random.normal(ks[3], (E, D, I), jnp.float32) * s, 'w3': jax.random.normal(ks[4], (E, I, D), jnp.float32) * s, 'ws1': jax.random.normal(ks[5], (SI, D), jnp.float32) * s, 'ws2': jax.random.normal(ks[6], (D, SI), jnp.float32) * s, 'ws3': jax.random.normal(ks[7], (SI, D), jnp.float32) * s}
    _L0_ffn_all = _L0_ffn_setup()
    _L0_ffn_in = {k: v for k, v in _L0_ffn_all.items() if k in ('gate_w', 'gate_b', 'w1', 'w2', 'w3', 'ws1', 'ws2', 'ws3')}
    del _L0_ffn_all

    def _L1_xattn_setup():
        import jax, jax.numpy as jnp
        import numpy as np
        key = jax.random.key(seed)
        ks = jax.random.split(key, 8)
        B, T, D, H = (4, 256, 128, 16)
        s_in = float(np.sqrt(2.0 / (D + 3 * D)))
        s_out = float(np.sqrt(2.0 / (D + D)))
        return {'query': jax.random.normal(ks[0], (B, T, D), jnp.float32), 'key': jax.random.normal(ks[1], (B, T, D), jnp.float32), 'value': jax.random.normal(ks[2], (B, T, D), jnp.float32), 'attention_bias': jax.random.normal(ks[3], (B, T, T), jnp.float32), 'in_proj_weight': jax.random.normal(ks[4], (3 * D, D), jnp.float32) * s_in, 'in_proj_bias': jnp.zeros((3 * D,), jnp.float32), 'out_w': jax.random.normal(ks[5], (D, D), jnp.float32) * s_out, 'out_b': jnp.zeros((D,), jnp.float32), 'head_scales': jnp.ones((H,), jnp.float32) + 0.1 * jax.random.normal(ks[6], (H,), jnp.float32), 'key_padding_mask': jnp.zeros((B, T), bool)}
    _L1_xattn_all = _L1_xattn_setup()
    _L1_xattn_in = {k: v for k, v in _L1_xattn_all.items() if k in ('in_proj_weight', 'in_proj_bias', 'out_w', 'out_b', 'head_scales')}
    del _L1_xattn_all

    def _L1_ffn_setup():
        import jax, jax.numpy as jnp
        import numpy as np
        from math import ceil
        CAPACITY_FACTOR = 2.0
        MIN_CAPACITY = 4
        key = jax.random.key(seed)
        ks = jax.random.split(key, 4)
        B, S, D, Di, E = (4, 256, 128, 512, 8)
        x = jax.random.normal(ks[0], (B, S, D), dtype=jnp.float32)
        Wr = jax.random.normal(ks[1], (D, E), dtype=jnp.float32) * D ** (-0.5)
        W1 = jax.random.normal(ks[2], (E, D, Di), dtype=jnp.float32) * D ** (-0.5)
        b1 = jnp.zeros((E, Di), dtype=jnp.float32)
        W2 = jax.random.normal(ks[3], (E, Di, D), dtype=jnp.float32) * Di ** (-0.5)
        b2 = jnp.zeros((E, D), dtype=jnp.float32)
        return {'x': x, 'Wr': Wr, 'W1': W1, 'b1': b1, 'W2': W2, 'b2': b2}
    _L1_ffn_all = _L1_ffn_setup()
    _L1_ffn_in = {k: v for k, v in _L1_ffn_all.items() if k in ('Wr', 'W1', 'b1', 'W2', 'b2')}
    del _L1_ffn_all
    return {'x': x, 'ctx_1024': ctx_1024, 'fside_BxSxS2_0': fside_BxSxS2_0, 'mask_1x1xSxS2_bk0': mask_1x1xSxS2_bk0, 'mask_BxS2_bf0': mask_BxS2_bf0, 'g_xattn': g_xattn, 'g_ffn': g_ffn, 'L0_xattn_w_q': _L0_xattn_in['w_q'], 'L0_xattn_w_k': _L0_xattn_in['w_k'], 'L0_xattn_w_v': _L0_xattn_in['w_v'], 'L0_xattn_w_o': _L0_xattn_in['w_o'], 'L0_ffn_gate_w': _L0_ffn_in['gate_w'], 'L0_ffn_gate_b': _L0_ffn_in['gate_b'], 'L0_ffn_w1': _L0_ffn_in['w1'], 'L0_ffn_w2': _L0_ffn_in['w2'], 'L0_ffn_w3': _L0_ffn_in['w3'], 'L0_ffn_ws1': _L0_ffn_in['ws1'], 'L0_ffn_ws2': _L0_ffn_in['ws2'], 'L0_ffn_ws3': _L0_ffn_in['ws3'], 'L1_xattn_in_proj_weight': _L1_xattn_in['in_proj_weight'], 'L1_xattn_in_proj_bias': _L1_xattn_in['in_proj_bias'], 'L1_xattn_out_w': _L1_xattn_in['out_w'], 'L1_xattn_out_b': _L1_xattn_in['out_b'], 'L1_xattn_head_scales': _L1_xattn_in['head_scales'], 'L1_ffn_Wr': _L1_ffn_in['Wr'], 'L1_ffn_W1': _L1_ffn_in['W1'], 'L1_ffn_b1': _L1_ffn_in['b1'], 'L1_ffn_W2': _L1_ffn_in['W2'], 'L1_ffn_b2': _L1_ffn_in['b2']}

def reference(x, ctx_1024, fside_BxSxS2_0, mask_1x1xSxS2_bk0, mask_BxS2_bf0, g_xattn, g_ffn, L0_xattn_w_q, L0_xattn_w_k, L0_xattn_w_v, L0_xattn_w_o, L0_ffn_gate_w, L0_ffn_gate_b, L0_ffn_w1, L0_ffn_w2, L0_ffn_w3, L0_ffn_ws1, L0_ffn_ws2, L0_ffn_ws3, L1_xattn_in_proj_weight, L1_xattn_in_proj_bias, L1_xattn_out_w, L1_xattn_out_b, L1_xattn_head_scales, L1_ffn_Wr, L1_ffn_W1, L1_ffn_b1, L1_ffn_W2, L1_ffn_b2):
    import jax
    import jax.numpy as jnp

    def _L0_xattn_ref(q, k, v, mask, w_q, w_k, w_v, w_o):
        import jax, jax.numpy as jnp
        import numpy as np
        D_MODEL = 128
        H = 16
        DK = D_MODEL // H
        B, S = (2, 256)
        NEG = -1000000000.0
        query = q @ w_q.T
        key_ = k @ w_k.T
        value = v @ w_v.T

        def split(x):
            return x.reshape(x.shape[0], x.shape[1], H, DK).transpose(0, 2, 1, 3)
        qh, kh, vh = (split(query), split(key_), split(value))
        scores = jnp.einsum('bhqd,bhkd->bhqk', qh, kh) / jnp.sqrt(jnp.float32(DK))
        scores = jnp.where(mask, scores, NEG)
        attn = jax.nn.softmax(scores, axis=-1)
        out = jnp.einsum('bhqk,bhkd->bhqd', attn, vh)
        out = out.transpose(0, 2, 1, 3).reshape(out.shape[0], -1, H * DK)
        return out @ w_o.T

    def _L0_ffn_ref(x, gate_w, gate_b, w1, w2, w3, ws1, ws2, ws3):
        import jax, jax.numpy as jnp
        import numpy as np
        E = 64
        K = 6
        CAP = 64
        ROUTE_SCALE = 1.0
        shape = x.shape
        D = shape[-1]
        xf = x.reshape(-1, D)
        T = xf.shape[0]
        scores = jax.nn.softmax(xf @ gate_w.T, axis=-1)
        _, idx = jax.lax.top_k(scores + gate_b, K)
        weights = jnp.take_along_axis(scores, idx, axis=1) * ROUTE_SCALE
        flat_e = idx.reshape(-1)
        order = jnp.argsort(flat_e)
        se = flat_e[order]
        counts = jnp.bincount(flat_e, length=E)
        starts = jnp.cumsum(counts) - counts
        pos = jnp.arange(T * K) - starts[se]
        tok = order // K
        xb = jnp.zeros((E, CAP, D), xf.dtype).at[se, pos].set(xf[tok], mode='drop')
        h = jax.nn.silu(jnp.einsum('ecd,eid->eci', xb, w1)) * jnp.einsum('ecd,eid->eci', xb, w3)
        yb = jnp.einsum('eci,edi->ecd', h, w2)
        valid = (pos < CAP).astype(xf.dtype)
        contrib = yb[se, jnp.minimum(pos, CAP - 1)]
        wf = weights.reshape(-1)[order] * valid
        y = jnp.zeros_like(xf).at[tok].add(contrib * wf[:, None])
        z = jax.nn.silu(xf @ ws1.T) * (xf @ ws3.T) @ ws2.T
        return (y + z).reshape(shape)

    def _L1_xattn_ref(query, key, value, attention_bias, in_proj_weight, in_proj_bias, out_w, out_b, head_scales, key_padding_mask):
        import jax, jax.numpy as jnp
        import numpy as np
        B, Tq, D = query.shape
        Tk = key.shape[1]
        H = head_scales.shape[0]
        hd = D // H
        scaling = 1.0 / np.sqrt(hd)
        qw, kw, vw = jnp.split(in_proj_weight, 3, axis=0)
        qb, kb, vb = jnp.split(in_proj_bias, 3)
        q = (query @ qw.T + qb).reshape(B, Tq, H, hd).transpose(0, 2, 1, 3)
        k = (key @ kw.T + kb).reshape(B, Tk, H, hd).transpose(0, 2, 1, 3)
        v = (value @ vw.T + vb).reshape(B, Tk, H, hd).transpose(0, 2, 1, 3)
        scores = jnp.einsum('bhqd,bhkd->bhqk', q, k) * scaling
        scores = scores + attention_bias[:, None, :, :]
        scores = jnp.where(key_padding_mask[:, None, None, :], -jnp.inf, scores)
        attn = jax.nn.softmax(scores, axis=-1)
        out = jnp.einsum('bhqk,bhkd->bhqd', attn, v)
        out = out * head_scales[None, :, None, None]
        out = out.transpose(0, 2, 1, 3).reshape(B, Tq, D)
        return out @ out_w.T + out_b

    def _L1_ffn_ref(x, Wr, W1, b1, W2, b2):
        import jax, jax.numpy as jnp
        import numpy as np
        from math import ceil
        CAPACITY_FACTOR = 2.0
        MIN_CAPACITY = 4
        B, S, D = x.shape
        E = Wr.shape[1]
        N = B * S
        k = max(MIN_CAPACITY, ceil(N * CAPACITY_FACTOR / E))
        xt = x.reshape(N, D)
        scores = jax.nn.softmax(xt @ Wr, axis=-1)
        G, idx = jax.lax.top_k(scores.T, k)
        X_in = xt[idx]
        h = jax.nn.gelu(jnp.einsum('ekd,edh->ekh', X_in, W1) + b1[:, None, :], approximate=False)
        X_e = jnp.einsum('ekh,ehd->ekd', h, W2) + b2[:, None, :]
        contrib = (G[..., None] * X_e).reshape(E * k, D)
        out = jnp.zeros((N, D), dtype=x.dtype).at[idx.reshape(-1)].add(contrib)
        return out.reshape(B, S, D)
    x = x + jnp.tanh(g_xattn[0]) * _L0_xattn_ref(_layernorm(x, axis=-1), ctx_1024, ctx_1024, mask_1x1xSxS2_bk0, L0_xattn_w_q, L0_xattn_w_k, L0_xattn_w_v, L0_xattn_w_o)
    x = x + jnp.tanh(g_ffn[0]) * _L0_ffn_ref(_layernorm(x, axis=-1), L0_ffn_gate_w, L0_ffn_gate_b, L0_ffn_w1, L0_ffn_w2, L0_ffn_w3, L0_ffn_ws1, L0_ffn_ws2, L0_ffn_ws3)
    x = x + jnp.tanh(g_xattn[1]) * _L1_xattn_ref(_layernorm(x, axis=-1), ctx_1024, ctx_1024, fside_BxSxS2_0, L1_xattn_in_proj_weight, L1_xattn_in_proj_bias, L1_xattn_out_w, L1_xattn_out_b, L1_xattn_head_scales, mask_BxS2_bf0)
    x = x + jnp.tanh(g_ffn[1]) * _L1_ffn_ref(_layernorm(x, axis=-1), L1_ffn_Wr, L1_ffn_W1, L1_ffn_b1, L1_ffn_W2, L1_ffn_b2)
    return x

_drawn_inputs = setup_inputs


def setup_inputs(seed=0):
    import zlib

    import numpy as np

    out = dict(_drawn_inputs(seed))
    spreads = {'g_ffn': (-1.0, 0.6),
     'L0_ffn_gate_b': (0.0, 0.8),
     'L1_xattn_in_proj_bias': (0.0, 0.1),
     'L1_xattn_out_b': (0.0, 0.1),
     'L1_ffn_b1': (0.0, 0.417),
     'L1_ffn_b2': (0.0, 0.277)}
    factors = {'L0_ffn_gate_w': 8.0,
     'L0_ffn_w1': 8.0,
     'L0_ffn_w2': 8.0,
     'L0_ffn_w3': 8.0,
     'L0_ffn_ws1': 7.472,
     'L0_ffn_ws2': 6.972,
     'L0_ffn_ws3': 7.069,
     'L1_xattn_head_scales': 3.999}
    for name, (base, spread) in spreads.items():
        noise = np.random.default_rng([zlib.crc32(name.encode()), seed]).standard_normal(out[name].shape)
        drawn = base * np.exp(spread * noise) if base else spread * noise
        out[name] = jnp.asarray(drawn.astype(out[name].dtype))
    for name, factor in factors.items():
        out[name] = (out[name] * factor).astype(out[name].dtype)
    return out
```

```python
from contextlib import ExitStack

import concourse.bass as bass
from concourse import mybir

F32 = mybir.dt.float32
BF16 = mybir.dt.bfloat16
U32 = mybir.dt.uint32
I32 = mybir.dt.int32
U8 = mybir.dt.uint8
ALU = mybir.AluOpType
ACT = mybir.ActivationFunctionType
AX = mybir.AxisListType

B, S, D = 32, 128, 128
KV = 120
H, DK = 16, 8
G = 4
N = B * S
E0, K0, CAP, I0 = 64, 6, 64, 88
SI = 2 * I0
E1, I1 = 8, 512
K1 = N * 2 // E1
NOWHERE = 2 * E0 * CAP
EPS = 1e-5
NEG = -1e9
FAR = -1e30
BLOCKS = 6
ROWS = BLOCKS * DK
QK = S + KV
PAY0 = D + E0
PAY1 = D + E1


class Steps:

    def __init__(self, eng, sem, per_batch, b):
        self.eng, self.sem, self.per_batch, self.b, self.k = eng, sem, per_batch, b, 0

    def then(self, instruction, apart=False):
        self.k += 1
        instruction.then_inc(self.sem, 1)
        value = self.b * self.per_batch + self.k
        if apart:
            Apart.wait(self.eng, self.sem, value)
        else:
            self.eng.wait_ge(self.sem, value)

    def end(self):
        assert self.k == self.per_batch, (self.k, self.per_batch)


class Apart:

    set_up = None

    @classmethod
    def wait(cls, eng, event, value):
        if not isinstance(value, int) or value > 0:
            if not isinstance(value, int):
                eng.lower_val(value)
            eng.wait_ge(cls.set_up, 1)
            eng.wait_ge(event, value)


class Named:
    pass


def pipelined(eng, stage1, stage2, stage3, middle):
    middle(0, None, None, 0)
    middle(1, 0, None, 0)
    middle(2, 1, 0, 1)
    middle(3, 2, 1, 0)
    with eng.Fori(3, B - 4, 2) as i:
        for k in range(2):
            middle(i + (k + 1), i + k, i + (k - 1), 1 - k)
    middle(B - 2, B - 3, B - 4, 1)
    middle(B - 1, B - 2, B - 3, 0)
    middle(None, B - 1, B - 2, 1)
    middle(None, None, B - 1, 0)


def at(tile, b):
    if isinstance(b, int):
        return tile[:, b, :]
    return tile[:, bass.ds(b, 1), :].rearrange("p o d -> p (o d)")


def row(dram, b):
    if isinstance(b, int):
        return dram[b]
    return dram[bass.ds(b, 1)].rearrange("o p d -> (o p) d")


def setup_block(nc, t, d, sem, psum):
    loaded, consts, cleared, gates, zero_made = (sem(x) for x in (
        "weights_loaded", "constants_step", "places_cleared", "gates_ready", "zeros_ready"))
    vstep = sem("setup_vector_step")
    loads = [
        (t.wqT[0], d.wqT0), (t.wkT[0], d.wkT0), (t.wvT[0], d.wvT0), (t.woT[0], d.woT0),
        (t.wqT[1], d.wqT1), (t.wkT[1], d.wkT1), (t.wvT[1], d.wvT1), (t.woT[1], d.woT1),
        (t.gateT, d.gateT), (t.wrT, d.wrT), (t.ws13T, d.ws13T), (t.ws2T, d.ws2T),
        (t.qkvb, d.qkvb), (t.hs, d.hs),
        (t.outb, d.outb.partition_broadcast(128)), (t.gb, d.gb.partition_broadcast(128)),
        (t.graw, d.graw.partition_broadcast(128)),
        (t.mask_u8, d.mask0), (t.padT_u8, d.padT), (t.pad_u8, d.pad.partition_broadcast(128)),
    ]
    with nc.Block() as block:
        @block.sync
        def _(sp):
            for q in range(8):
                sp.dma_start(t.X[:, 4 * q:4 * q + 4, :],
                             d.x[4 * q:4 * q + 4].rearrange("b p d -> p b d")).then_inc(loaded, 16)
            for tile, src in loads:
                sp.dma_start(tile[:], src).then_inc(loaded, 16)
            sp.wait_ge(zero_made, 1)
            for q in range(4):
                sp.dma_start(d.places[q * 1024:(q + 1) * 1024, :].rearrange("(k p) w -> p k w", p=128),
                             t.zeros[:].rearrange("p (k w) -> p k w", w=PAY0)).then_inc(cleared, 16)
            sp.wait_ge(cleared, 64)
            sp.sem_inc(Apart.set_up, 1)
            sp.wait_ge(loaded, 16 * (8 + len(loads)))

        @block.gpsimd
        def _(pool):
            c = Steps(pool, consts, 0, 0)
            select = lambda out, op, fill, base, pattern, cm: c.then(nc.gpsimd.affine_select(
                out=out, in_=out, compare_op=op, fill=fill, base=base, pattern=pattern, channel_multiplier=cm))
            nc.gpsimd.memset(t.zeros[:], 0.0).then_inc(zero_made, 1)
            for tile in (t.ident, t.identb):
                c.then(nc.gpsimd.memset(tile[:], 0.0))
                select(tile[:], ALU.not_equal, 1.0, 0, [[-1, 128]], 1)
            c.then(nc.gpsimd.memset(t.before[:], 1.0))
            select(t.before[:], ALU.is_gt, 0.0, 0, [[1, 128]], -1)
            c.then(nc.gpsimd.memset(t.onesb[:], 1.0))
            c.then(nc.gpsimd.memset(t.pick[:], 0.0))
            for first in (0, 32):
                select(t.pick[:], ALU.not_equal, 1.0, -first, [[-1, H], [0, KV]], 1)
            c.then(nc.gpsimd.memset(t.headcols[:], 0.0))
            for i in range(G):
                c.then(nc.gpsimd.memset(t.headcols[:, i, i * DK:(i + 1) * DK], 1.0))
            c.then(nc.gpsimd.iota(t.iota_e[:], pattern=[[-CAP, E0]], base=NOWHERE, channel_multiplier=0))
            c.then(nc.gpsimd.tensor_copy(t.lastplace[:], t.iota_e[:]))
            c.then(nc.gpsimd.memset(t.minus_half[:], -0.5))
            for tile in (t.same, t.earlier):
                c.then(nc.gpsimd.memset(tile[:], 1.0))
                v = tile[:].rearrange("p (g r) -> p g r", g=4)
                select(v, ALU.is_ge, 0.0, 0, [[-32, 4], [0, 32]], 1)
                select(v, ALU.is_ge, 0.0, 31, [[32, 4], [0, 32]], -1)
            select(t.earlier[:], ALU.is_gt, 0.0, 0, [[1, 128]], -1)
            c.then(nc.gpsimd.iota(t.iota_r[:], pattern=[[128, K1 // 128]], base=0, channel_multiplier=1))
            c.then(nc.gpsimd.tensor_copy(t.rank[:], t.iota_r[:]))
            c.then(nc.gpsimd.iota(t.iota_s[:], pattern=[[1, K1]], base=0, channel_multiplier=0))
            c.then(nc.gpsimd.tensor_copy(t.slotno[:], t.iota_s[:]))
            c.then(nc.gpsimd.iota(t.iota_t[:], pattern=[[0, 1]], base=0, channel_multiplier=128))
            c.then(nc.gpsimd.tensor_copy(t.tile_start[:], t.iota_t[:]))
            for g in range(1, 4):
                c.then(nc.gpsimd.tensor_scalar(t.tile_start[32 * g:32 * g + 32, :], t.tile_start[32 * g:32 * g + 32, :],
                                               float(-N * g), None, ALU.add))
            for tile in (t.Qs, t.Ks, t.nmT, t.nm, t.Vb, t.sacc):
                c.then(nc.gpsimd.memset(tile[:], 0.0))

        @block.scalar
        def _(act):
            act.wait_ge(loaded, 16 * (8 + len(loads)))
            nc.scalar.activation(t.gate[:], t.graw[:], ACT.Tanh).then_inc(gates, 1)

        @block.vector
        def _(dve):
            c = Steps(dve, vstep, 0, 0)
            dve.wait_ge(loaded, 16 * (8 + len(loads)))
            c.then(nc.vector.tensor_scalar(t.mask0[:], t.mask_u8[:], -NEG, NEG, ALU.mult, ALU.add))
            c.then(nc.vector.tensor_copy(t.mask_f[:], t.mask_u8[:]))
            c.then(nc.vector.tensor_reduce(t.rowany[:], t.mask_f[:], AX.X, ALU.max))
            c.then(nc.vector.tensor_scalar(t.padfar[:], t.pad_u8[:], FAR, None, ALU.mult))
            c.then(nc.vector.tensor_scalar(t.padinf[:], t.padT_u8[:], -3e38, 10.0, ALU.mult, ALU.mult))
            c.then(nc.vector.tensor_scalar(t.qbs[:], t.qkvb[:, 0:1], DK ** -0.5, None, ALU.mult))
            dve.wait_ge(gates, 1)
            c.then(nc.vector.tensor_scalar(t.outbg[:], t.outb[:], t.gate[:, 2:3], None, ALU.mult))


def attention_block(nc, L, t, d, sem_, ps):

    def sem(name):
        return sem_(f"{name}_{L}")

    ev = Named()
    ev.ctx_loaded = sem("ctx_loaded")
    ev.stored = sem("stored")
    ev.bounced = sem("bounced")
    ev.stats1 = sem("stats1")
    ev.rstd1 = sem("rstd1")
    ev.xn = sem("xn")
    ev.xT = sem("xT")
    ev.xTc = sem("xTc")
    ev.qkv = sem("qkv")
    ev.qf = sem("qf")
    ev.hi = sem("hi")
    ev.parts = sem("parts")
    ev.vb = sem("vb")
    ev.scores = sem("scores")
    ev.maxed = sem("maxed")
    ev.nm = sem("nm")
    ev.nmT = sem("nmT")
    ev.nmTc = sem("nmTc")
    ev.scoresT = sem("scoresT")
    ev.exped = sem("exped")
    ev.pv = sem("pv")
    ev.oT = sem("oT")
    ev.proj = sem("proj")
    ev.resid = sem("resid")
    ev.stats2 = sem("stats2")
    ev.rstd2 = sem("rstd2")
    ev.xn2 = sem("xn2")
    ev.xT2 = sem("xT2")
    ev.xT2c = sem("xT2c")
    ev.logits = sem("logits")
    ev.negmax = sem("negmax")
    ev.rexp = sem("rexp")
    ev.v1 = sem("v1")
    ev.v2 = sem("v2")
    ev.v3 = sem("v3")
    ev.p1 = sem("p1")
    ev.p2 = sem("p2")
    if L == 0:
        ev.scattered = sem("scattered")
        ev.xkept = sem("xkept")
        ev.sel = sem("sel")
        ev.sacc = sem("sacc")
        ev.pos = sem("pos")
        ev.slot = sem("slot")
    else:
        ev.bias_loaded = sem("bias_loaded")
        ev.gathered = sem("gathered")
        ev.rows_stored = sem("rows_stored")
        ev.payload = sem("payload")
        ev.bias_parts = sem("bias_parts")
        ev.ysum = sem("ysum")
        ev.slots_fetched = sem("slots_fetched")
        ev.cleared = sem("cleared")
        ev.p3 = sem("p3")
    wq, wk, wv, wo = t.wqT[L], t.wkT[L], t.wvT[L], t.woT[L]
    M1, M2, PV, SM = ps[0], ps[1], ps[2], ps[3]
    SA, TA = ps[4:6], ps[6:8]
    xT_ps, qk_ps, v_ps = M1[:, 0:S], M1[:, S:S + QK], M1[0:KV, S + QK:S + QK + D]
    o_ps, xT2_ps, lg_ps = M2[:, 0:D], M2[:, 128:256], M2[:, 256:256 + (E0 if L == 0 else E1)]
    pos_ps = M2[:, 320:384]
    nmT_ps = M1[0:48, 0:S // 2].bitcast(BF16)
    sc_w = E0 if L == 0 else E1
    attn_gate = t.gate[:, 2 * L:2 * L + 1]
    ffn_gate = t.gate[:, 1:2]

    def used(eng, event, value):
        if not isinstance(value, int) or value > 0:
            eng.wait_ge(event, value)

    with nc.Block() as block:
        @block.sync
        def _(sp):
            def load(n, u):
                used(sp, ev.ctx_loaded, n * 16)
                used(sp, ev.qkv, n - 1)
                sp.dma_start(t.ctx[:, u, :], row(d.ctxT, n)).then_inc(ev.ctx_loaded, 16)
                if L == 1:
                    used(sp, ev.bias_loaded, n * 16)
                    used(sp, ev.bias_parts, n - 1)
                    sp.dma_start(t.fb[:, u, :], row(d.fside, n)).then_inc(ev.bias_loaded, 16)

            def bounce(n, u):
                Apart.wait(sp, ev.parts, n + 1)
                used(sp, ev.bounced, 32 * n)
                qp, kp = t.parts[:, u, :, 0:S], t.parts[:, u, :, S:QK]
                sc = d.scrq.rearrange("(b c) q -> c b q", b=BLOCKS), d.scrk.rearrange("(b c) q -> c b q", b=BLOCKS)
                for first, parts in ((0, 3), (3, 2), (5, 1)):
                    sp.dma_start(sc[0][:, first:first + parts, :], qp[:, 0:parts, :]).then_inc(ev.stored, 16)
                for part, (first, times) in enumerate(((0, 3), (3, 2), (5, 1))):
                    sp.dma_start(sc[1][:, first:first + times, :],
                                 kp[:, part:part + 1, :].broadcast_to([D, times, KV])).then_inc(ev.stored, 16)
                Apart.wait(sp, ev.stored, 96 * (n + 1))
                used(sp, ev.scoresT, G * (n - 1))
                for stack, scr in ((t.Qs, d.scrq), (t.Ks, d.scrk)):
                    sp.dma_start(stack[0:ROWS, u, :, :].rearrange("p h q -> p (h q)"),
                                 scr.rearrange("(r h) q -> r (h q)", h=H)).then_inc(ev.bounced, 16)

            def store_rows(p, u):
                if L == 1:
                    Apart.wait(sp, ev.payload, p + 1)
                    used(sp, ev.rows_stored, 32 * p)
                    sp.dma_start(row(d.rows, p), t.payload[:, u, 0:PAY1]).then_inc(ev.rows_stored, 16)
                    sp.dma_start(row(d.out, p), at(t.X, p)).then_inc(ev.rows_stored, 16)

            def middle(n, i, p, u):
                if n is not None and not (isinstance(n, int) and n == 0):
                    load(n, 1 - u)
                    bounce(n, 1 - u)
                elif n is not None:
                    load(n, 0)
                    bounce(n, 0)
                if p is not None:
                    store_rows(p, 1 - u)

            pipelined(sp, None, None, None, middle)
            if L == 1:
                sp.wait_ge(ev.rows_stored, 32 * B)

        @block.tensor
        def _(pe):
            def transpose_x(n, u):
                pe.wait_ge(ev.xn, n + 1)
                used(pe, ev.vb, n)
                used(pe, ev.nmTc, n - 1)
                nc.tensor.transpose(xT_ps, t.xn[:, u, :], t.ident[:]).then_inc(ev.xT, 1)

            def project(n, u):
                pe.wait_ge(ev.xTc, n + 1)
                pe.wait_ge(ev.ctx_loaded, 16 * (n + 1))
                nc.tensor.matmul(qk_ps[:, 0:S], wq[:], t.xnT[:, u, :], start=True, stop=True)
                nc.tensor.matmul(qk_ps[:, S:QK], wk[:], t.ctx[:, u, :], start=True, stop=True)
                nc.tensor.matmul(v_ps, t.ctx[:, u, :], wv[:], start=True, stop=True).then_inc(ev.qkv, 1)

            def scores(i, u, g):
                if g == 0:
                    pe.wait_ge(ev.bounced, 32 * (i + 1))
                    if L == 1:
                        pe.wait_ge(ev.bias_parts, i + 1)
                used(pe, ev.maxed, G * i + g - 1)
                bank = SA[g % 2][:, 0:G * KV].rearrange("p (j k) -> p j k", j=G)
                parts = [t.mask0[:]] if L == 0 else [t.bp[:, u, 0, :], t.bp[:, u, 1, :]]
                for k, part in enumerate(parts):
                    nc.tensor.matmul(bank, t.identb[:], part.unsqueeze(1).broadcast_to([S, G, KV]),
                                     start=(k == 0), stop=False)
                for j in range(G):
                    mm = nc.tensor.matmul(bank[:, j, :], t.Qs[:, u, G * j + g, :], t.Ks[:, u, G * j + g, :],
                                          start=False, stop=(j == G - 1))
                mm.then_inc(ev.scores, 1)

            def transpose_max(i, u):
                Apart.wait(pe, ev.nm, i + 1)
                if not isinstance(i, int) or i + 1 < B:
                    pe.wait_ge(ev.vb, i + 2)
                nc.tensor.transpose(nmT_ps, t.nm[:, u, :], t.identb[:]).then_inc(ev.nmT, 1)

            def scores_T(i, u, g):
                if g == 0:
                    pe.wait_ge(ev.nmTc, i + 1)
                used(pe, ev.exped, G * i + g - 1)
                bank = TA[g % 2][0:KV, :].rearrange("p (j q) -> p j q", j=G)
                parts = [t.mask0[:]] if L == 0 else [t.bp[:, u, k, :] for k in range(3)]
                for k, part in enumerate(parts):
                    nc.tensor.matmul(bank, part, t.identb[:].unsqueeze(1).broadcast_to([S, G, S]),
                                     start=(k == 0), stop=False)
                for j in range(G):
                    nc.tensor.matmul(bank[:, j, :], t.Ks[:, u, G * j + g, :], t.Qs[:, u, G * j + g, :],
                                     start=False, stop=False)
                    mm = nc.tensor.matmul(bank[:, j, :], t.pick[:, G * g + j, :], t.nmT[:, u, :],
                                          start=False, stop=(j == G - 1))
                mm.then_inc(ev.scoresT, 1)

            def values(i, u, g):
                pe.wait_ge(ev.exped, G * i + g + 1)
                if g == 0:
                    pe.wait_ge(ev.vb, i + 1)
                    used(pe, ev.oT, i)
                for out, col in ((PV, None), (SM, t.headcols)):
                    for j in range(G):
                        w = t.Vb[0:KV, u, j, 32 * g:32 * g + 32] if col is None else col[0:KV, g, :]
                        mm = nc.tensor.matmul(out[32 * j:32 * j + 32, 0:S], w,
                                              t.PT[0:KV, g, S * j:S * j + S], start=(g == 0), stop=(g == G - 1))
                mm.then_inc(ev.pv, 1)

            def project_out(p, u):
                pe.wait_ge(ev.oT, p + 1)
                used(pe, ev.slot if L == 0 else ev.rexp, p)
                nc.tensor.matmul(o_ps, t.oT[:, u, :], wo[:], start=True, stop=True).then_inc(ev.proj, 1)

            def transpose_x2(p, u):
                pe.wait_ge(ev.xn2, p + 1)
                nc.tensor.transpose(xT2_ps, t.payload[:, u, 0:D], t.ident[:]).then_inc(ev.xT2, 1)

            def logits(p, u):
                pe.wait_ge(ev.xT2c, p + 1)
                w = t.gateT if L == 0 else t.wrT
                nc.tensor.matmul(lg_ps, t.xT2[:, u, :], w[:], start=True, stop=True).then_inc(ev.logits, 1)

            def positions(p, u):
                pe.wait_ge(ev.sel, p + 1)
                used(pe, ev.sacc, p)
                pe.wait_ge(ev.rexp, p + 1)
                nc.tensor.matmul(pos_ps, t.before[:], t.sel[:, u, :], start=True, stop=False)
                nc.tensor.matmul(pos_ps, t.onesb[:], t.sacc[:, u, :], start=False, stop=True).then_inc(ev.pos, 1)

            def middle(n, i, p, u):
                w = 1 - u if i is not None or p is not None else 0
                if p is not None:
                    project_out(p, w)
                if i is not None:
                    scores(i, u, 0)
                    scores(i, u, 1)
                if p is not None:
                    transpose_x2(p, w)
                if n is not None:
                    transpose_x(n, w)
                if i is not None:
                    scores(i, u, 2)
                if n is not None:
                    project(n, w)
                if i is not None:
                    scores(i, u, 3)
                if p is not None:
                    logits(p, w)
                if i is not None:
                    transpose_max(i, u)
                    scores_T(i, u, 0)
                    scores_T(i, u, 1)
                if p is not None and L == 0:
                    positions(p, w)
                if i is not None:
                    values(i, u, 0)
                    scores_T(i, u, 2)
                    values(i, u, 1)
                    scores_T(i, u, 3)
                    values(i, u, 2)
                    values(i, u, 3)

            pipelined(pe, None, None, None, middle)

        @block.scalar
        def _(act):
            def middle(n, i, p, u):
                w = 1 - u if i is not None or p is not None else 0
                if p is not None:
                    act.wait_ge(ev.xT2, p + 1)
                    used(act, ev.logits, p - 1)
                    if L == 0:
                        used(act, ev.xkept, p - 1)
                    nc.scalar.activation(t.xT2[:, w, :], xT2_ps, ACT.Copy).then_inc(ev.xT2c, 1)
                if n is not None:
                    act.wait_ge(ev.xT, n + 1)
                    used(act, ev.qkv, n - 1)
                    nc.scalar.activation(t.xnT[:, w, :], xT_ps, ACT.Copy).then_inc(ev.xTc, 1)
                    act.wait_ge(ev.qkv, n + 1)
                    used(act, ev.parts, n - 1)
                    used(act, ev.stored, 96 * (n - 1))
                    qb, kb = (0.0, 0.0) if L == 0 else (t.qbs[:], t.qkvb[:, 1:2])
                    nc.scalar.activation(t.qkf[:, w, 0:S], qk_ps[:, 0:S], ACT.Identity, bias=qb,
                                         scale=DK ** -0.5).then_inc(ev.qf, 1)
                    nc.scalar.activation(t.qkf[:, w, S:QK], qk_ps[:, S:QK], ACT.Identity, bias=kb).then_inc(ev.qf, 1)
                    used(act, ev.pv, G * (n - 1))
                    nc.scalar.activation(
                        t.Vb[0:KV, w, :, :].rearrange("p j (i x) -> p j i x", x=40)[:, :, :, 0:DK],
                        v_ps.rearrange("p (j i d) -> p j i d", j=G, i=G), ACT.Copy).then_inc(ev.vb, 1)
                    act.wait_ge(ev.qf, 2 * n + 2)
                    nc.scalar.activation(t.parts[:, w, 0, :], t.qkf[:, w, :], ACT.Copy).then_inc(ev.hi, 1)
                if i is not None:
                    act.wait_ge(ev.nmT, i + 1)
                    used(act, ev.scoresT, G * (i - 1))
                    nc.scalar.activation(t.nmT[0:48, u, :], nmT_ps, ACT.Copy).then_inc(ev.nmTc, 1)
                if p is not None:
                    act.wait_ge(ev.negmax, p + 1)
                    nc.scalar.activation(t.ex[:, w, 0:sc_w], lg_ps, ACT.Exp, bias=t.negmax[:, w, :],
                                         accum_out=t.exsum[:, w, :]).then_inc(ev.rexp, 1)
                if i is not None:
                    for g in range(G):
                        Apart.wait(act, ev.scoresT, G * i + g + 1)
                        Apart.wait(act, ev.pv, G * (i - 1) + g + 1)
                        if L == 0:
                            pad = 0.0
                        elif isinstance(i, int):
                            pad = t.padinf[0:KV, i:i + 1]
                        else:
                            pad = t.padinf[0:KV, bass.ds(i, 1)]
                        nc.scalar.activation(t.PT[0:KV, g, :], TA[g % 2][0:KV, :], ACT.Exp,
                                             bias=pad).then_inc(ev.exped, 1)

            pipelined(act, None, None, None, middle)

        @block.gpsimd
        def _(pool):
            def rstd(b, u, k, stats, ready, stepsem):
                Apart.wait(pool, stats, b + 1)
                queries0 = L == 0 and k == 0
                c = Steps(pool, stepsem, 2 if queries0 else 1, b)
                c.then(nc.gpsimd.tensor_scalar(t.rs[:, k, u, :], t.mv[:, k, u, 1:2], EPS, None, ALU.add))
                power = nc.gpsimd.tensor_tensor(t.rstd[:, k, u, :], t.rs[:, k, u, :], t.minus_half[:], ALU.pow)
                if queries0:
                    c.then(power)
                    power = nc.gpsimd.tensor_tensor(t.rstd[:, k, u, :], t.rstd[:, k, u, :], t.rowany[:], ALU.mult)
                power.then_inc(ready, 1)
                c.end()

            def split_bias(n, u):
                c = Steps(pool, ev.p3, 4, n)
                pool.wait_ge(ev.bias_loaded, 16 * (n + 1))
                used(pool, ev.scoresT, G * (n - 1))
                c.then(nc.gpsimd.tensor_tensor(t.fb2[:, 0, :], t.fb[:, u, :], at(t.padfar_rows, n), ALU.add), apart=True)
                c.then(nc.gpsimd.tensor_copy(t.bp[:, u, 0, :], t.fb2[:, 0, :]))
                c.then(nc.gpsimd.tensor_tensor(t.fb2[:, 1, :], t.fb2[:, 0, :], t.bp[:, u, 0, :], ALU.subtract),
                       apart=True)
                c.then(nc.gpsimd.tensor_copy(t.bp[:, u, 1, :], t.fb2[:, 1, :]))
                nc.gpsimd.tensor_tensor(t.bp[:, u, 2, :], t.fb2[:, 1, :], t.bp[:, u, 1, :],
                                        ALU.subtract).then_inc(ev.bias_parts, 1)
                c.end()

            def gather(b, u):
                used(pool, ev.gathered, 16 * K0 * b)
                Apart.wait(pool, ev.ysum, b - 1)
                nc.gpsimd.tensor_copy(t.slotg[:, u, :], at(t.slots, b)).then_inc(ev.slots_fetched, 1)
                nc.gpsimd.memset(t.yrows[:, u, :, :], 0.0).then_inc(ev.cleared, 1)
                Apart.wait(pool, ev.slots_fetched, b + 1)
                Apart.wait(pool, ev.cleared, b + 1)
                for j in range(K0):
                    nc.gpsimd.indirect_dma_start(
                        out=t.yrows[:, u, j, :], out_offset=None, in_=d.yplaces,
                        in_offset=bass.IndirectOffsetOnAxis(ap=t.slotg[:, u, j:j + 1], axis=0),
                        bounds_check=E0 * CAP - 1, oob_is_err=False).then_inc(ev.gathered, 16)

            def keep(p, u):
                Apart.wait(pool, ev.xT2c, p + 1)
                nc.gpsimd.tensor_copy(at(t.XT, p), t.xT2[:, u, :]).then_inc(ev.xkept, 1)

            def count(p, u):
                pool.wait_ge(ev.sel, p + 1)
                used(pool, ev.pos, p)
                used(pool, ev.sacc, p)
                nc.gpsimd.tensor_tensor(t.sacc[:, 1 - u, :], t.sacc[:, u, :], t.sel[:, u, :],
                                        ALU.add).then_inc(ev.sacc, 1)

            def scatter(p, u):
                pool.wait_ge(ev.slot, p + 1)
                Apart.wait(pool, ev.scattered, 16 * K0 * p)
                for j in range(K0):
                    nc.gpsimd.indirect_dma_start(
                        out=d.places, out_offset=bass.IndirectOffsetOnAxis(ap=t.slot[:, u, j:j + 1], axis=0),
                        in_=t.payload[:, u, 0:PAY0], in_offset=None,
                        bounds_check=E0 * CAP - 1, oob_is_err=False).then_inc(ev.scattered, 16)

            def middle(n, i, p, u):
                w = 1 - u if i is not None or p is not None else 0
                if L == 1 and n is not None and isinstance(n, int) and n == 0:
                    gather(0, 0)
                if p is not None:
                    rstd(p, w, 1, ev.stats2, ev.rstd2, ev.p2)
                if n is not None:
                    rstd(n, w, 0, ev.stats1, ev.rstd1, ev.p1)
                    if L == 1:
                        split_bias(n, w)
                        if not isinstance(n, int) or n + 1 < B:
                            gather(n + 1, 1 - w)
                if p is not None and L == 0:
                    keep(p, w)
                    count(p, w)
                    scatter(p, w)

            pipelined(pool, None, None, None, middle)
            if L == 0:
                pool.wait_ge(ev.scattered, 16 * K0 * B)

        @block.vector
        def _(dve):
            ve = nc.vector

            def stats(b, u, k, event, c):
                c.then(ve.bn_stats(t.st[:, k, :], at(t.X, b)), apart=True)
                ve.bn_aggr(t.mv[:, k, u, :], t.st[:, k, :]).then_inc(event, 1)

            def add_experts(n, u, c):
                dve.wait_ge(ev.gathered, 16 * K0 * (n + 1))
                ve.tensor_reduce(t.ysum[:], t.yrows[:, u, :, :].rearrange("p j d -> p d j"), AX.X,
                                 ALU.add).then_inc(ev.ysum, 1)
                dve.wait_ge(ev.ysum, n + 1)
                c.then(ve.scalar_tensor_tensor(at(t.X, n), t.ysum[:], ffn_gate, at(t.X, n), ALU.mult, ALU.add),
                       apart=True)

            def norm1(n, u, c):
                dve.wait_ge(ev.stats1, n + 1)
                dve.wait_ge(ev.rstd1, n + 1)
                used(dve, ev.xT, n - 1)
                ve.tensor_scalar(t.xn[:, u, :], at(t.X, n), t.mv[:, 0, u, 0:1], t.rstd[:, 0, u, :],
                                 ALU.subtract, ALU.mult).then_inc(ev.xn, 1)
                if L == 1:
                    dve.wait_ge(ev.xn, n + 1)
                    c.then(ve.tensor_tensor(at(t.X, n), at(t.X, n), t.outbg[:], ALU.add))

            def split(n, u, c):
                dve.wait_ge(ev.hi, n + 1)
                c.then(ve.tensor_tensor(t.rest[:], t.qkf[:, u, :], t.parts[:, u, 0, :], ALU.subtract))
                c.then(ve.tensor_copy(t.parts[:, u, 1, :], t.rest[:]))
                ve.tensor_tensor(t.parts[:, u, 2, :], t.rest[:], t.parts[:, u, 1, :],
                                 ALU.subtract).then_inc(ev.parts, 1)

            def head_max(i, u, g):
                dve.wait_ge(ev.scores, G * i + g + 1)
                ve.tensor_reduce(t.mx[:, G * g:G * g + G],
                                 SA[g % 2][:, 0:G * KV].rearrange("p (j k) -> p j k", j=G),
                                 AX.X, ALU.max).then_inc(ev.maxed, 1)

            def negate_max(i, u, c):
                dve.wait_ge(ev.maxed, G * (i + 1))
                used(dve, ev.nmT, i - 1)
                c.then(ve.tensor_scalar(t.nm[:, u, 0:H], t.mx[:], -1.0, None, ALU.mult))
                ve.scalar_tensor_tensor(t.nm[:, u, 32:32 + H], t.mx[:], -1.0, t.nm[:, u, 0:H], ALU.mult,
                                        ALU.subtract).then_inc(ev.nm, 1)
                dve.wait_ge(ev.nm, i + 1)

            def normalise(i, u, c):
                dve.wait_ge(ev.pv, G * (i + 1))
                c.then(ve.reciprocal(t.rsum[:], SM[:, 0:S]))
                used(dve, ev.proj, i - 1)
                scaled = ve.tensor_tensor(t.oT[:, u, :], PV[:, 0:S], t.rsum[:], ALU.mult)
                if L == 1:
                    c.then(scaled)
                    scaled = ve.tensor_scalar(t.oT[:, u, :], t.oT[:, u, :], t.qkvb[:, 2:3], t.hs[:],
                                              ALU.add, ALU.mult)
                scaled.then_inc(ev.oT, 1)

            def residual(p, u, c):
                dve.wait_ge(ev.proj, p + 1)
                ve.scalar_tensor_tensor(at(t.X, p), o_ps, attn_gate, at(t.X, p), ALU.mult,
                                        ALU.add).then_inc(ev.resid, 1)
                Apart.wait(dve, ev.resid, p + 1)
                stats(p, u, 1, ev.stats2, c)

            def norm2(p, u):
                dve.wait_ge(ev.stats2, p + 1)
                dve.wait_ge(ev.rstd2, p + 1)
                if L == 0:
                    used(dve, ev.scattered, 16 * K0 * (p - 1))
                    used(dve, ev.xT2, p - 1)
                else:
                    used(dve, ev.rows_stored, 32 * (p - 1))
                ve.tensor_scalar(t.payload[:, u, 0:D], at(t.X, p), t.mv[:, 1, u, 0:1], t.rstd[:, 1, u, :],
                                 ALU.subtract, ALU.mult).then_inc(ev.xn2, 1)

            def router_max(p, u, c):
                dve.wait_ge(ev.logits, p + 1)
                c.then(ve.tensor_reduce(t.lmax[:], lg_ps, AX.X, ALU.max))
                ve.tensor_scalar(t.negmax[:, u, :], t.lmax[:], -1.0, None, ALU.mult).then_inc(ev.negmax, 1)

            def router0(p, u, c):
                dve.wait_ge(ev.rexp, p + 1)
                c.then(ve.reciprocal(t.exrec[:], t.exsum[:, u, :]))
                c.then(ve.tensor_scalar(t.payload[:, u, D:PAY0], t.ex[:, u, :], t.exrec[:], None, ALU.mult))
                c.then(ve.tensor_tensor(t.biased[:], t.payload[:, u, D:PAY0], t.gb[:], ALU.add), apart=True)
                c.then(ve.max(t.top8[:], t.biased[:]))
                c.then(ve.tensor_scalar(t.above[:], t.biased[:], t.top8[:, K0 - 1:K0], 0.0, ALU.is_gt, ALU.add,
                                        accum_out=t.n_above[:]))
                c.then(ve.tensor_scalar(t.equal[:], t.biased[:], t.top8[:, K0 - 1:K0], None, ALU.is_equal))
                c.then(ve.tensor_tensor_scan(t.n_equal[:], t.equal[:], t.equal[:], 0.0, ALU.add, ALU.max))
                c.then(ve.tensor_scalar(t.wanted[:], t.n_above[:], -1.0, float(K0), ALU.mult, ALU.add))
                c.then(ve.scalar_tensor_tensor(t.equal[:], t.n_equal[:], t.wanted[:], t.equal[:], ALU.is_le, ALU.mult))
                ve.tensor_tensor(t.sel[:, u, :], t.above[:], t.equal[:], ALU.add).then_inc(ev.sel, 1)
                dve.wait_ge(ev.sel, p + 1)

            def place(p, u, c):
                dve.wait_ge(ev.pos, p + 1)
                c.then(ve.scalar_tensor_tensor(t.fits[:], pos_ps, float(CAP), t.sel[:, u, :], ALU.is_lt, ALU.mult))
                c.then(ve.tensor_tensor(t.back[:], t.lastplace[:], pos_ps, ALU.subtract))
                c.then(ve.tensor_tensor(t.back[:], t.back[:], t.fits[:], ALU.mult), apart=True)
                c.then(ve.max(t.top8b[:], t.back[:]))
                c.then(ve.tensor_scalar(t.slot[:, u, :], t.top8b[:], -1.0, float(NOWHERE), ALU.mult, ALU.add))
                ve.tensor_copy(at(t.slots, p), t.slot[:, u, :]).then_inc(ev.slot, 1)

            def router1(p, u, c):
                dve.wait_ge(ev.rexp, p + 1)
                c.then(ve.reciprocal(t.exrec[:], t.exsum[:, u, :]))
                c.then(ve.tensor_scalar(t.payload[:, u, D:PAY1], t.ex[:, u, 0:E1], t.exrec[:], None, ALU.mult))
                dst = t.scores1[:, :, p:p + 1] if isinstance(p, int) else t.scores1[:, :, bass.ds(p, 1)]
                ve.tensor_copy(dst.rearrange("p e o -> p (e o)"), t.payload[:, u, D:PAY1]).then_inc(ev.payload, 1)

            def middle(n, i, p, u):
                w = 1 - u if i is not None or p is not None else 0
                s1 = None if n is None else Steps(dve, ev.v1, 3 if L == 0 else 5, n)
                s2 = None if i is None else Steps(dve, ev.v2, 2 if L == 0 else 3, i)
                s3 = None if p is None else Steps(dve, ev.v3, 16 if L == 0 else 4, p)
                if p is not None:
                    residual(p, w, s3)
                if i is not None:
                    head_max(i, u, 0)
                if n is not None:
                    if L == 1:
                        add_experts(n, w, s1)
                    stats(n, w, 0, ev.stats1, s1)
                if i is not None:
                    head_max(i, u, 1)
                if p is not None:
                    norm2(p, w)
                if n is not None:
                    norm1(n, w, s1)
                if i is not None:
                    head_max(i, u, 2)
                    head_max(i, u, 3)
                    negate_max(i, u, s2)
                if n is not None:
                    split(n, w, s1)
                if p is not None:
                    router_max(p, w, s3)
                    (router0 if L == 0 else router1)(p, w, s3)
                    if L == 0:
                        place(p, w, s3)
                if i is not None:
                    normalise(i, u, s2)
                for c in (s1, s2, s3):
                    if c is not None:
                        c.end()

            pipelined(dve, None, None, None, middle)


def silu_gate(nc, dve, c, tmp, rec, out, h1, h3):
    c.then(nc.vector.tensor_scalar(tmp, tmp, 1.0, None, ALU.add))
    c.then(nc.vector.reciprocal(rec, tmp))
    c.then(nc.vector.tensor_tensor(rec, h1, rec, ALU.mult))
    return nc.vector.tensor_tensor(out, h3, rec, ALU.mult)


def experts0_block(nc, t, d, sem, ps):
    T4 = 4
    NB = B // T4
    GE = 8
    NG = E0 // GE
    (s_h, s_e, s_u, s_z, s_zadd, s_vs, r_w, r_x, r_T, r_Tc, r_h, r_e, r_u, r_y, r_yo, r_vs, r_wt, r_out) = (
        sem(f"mlp_{x}") for x in (
            "hidden", "exp", "gated", "out", "added", "vector_step",
            "weights_loaded", "places_loaded", "places_T", "places_T_copied", "expert_hidden", "expert_exp",
            "expert_gated", "expert_out", "expert_scaled", "expert_vector_step", "scores_loaded", "rows_out"))
    H1 = ps[0], ps[2]
    H3 = ps[1], ps[3]
    Y = ps[4], ps[5]
    TP = ps[6]

    def whole(x, n):
        return x if isinstance(x, int) else x

    def later(eng, event, value):
        if not isinstance(value, int) or value > 0:
            eng.wait_ge(event, value)

    def groups(eng, body, last):
        body(0, 0)
        body(1, 1)
        body(2, 0)
        with eng.Fori(3, NG - 2, 2) as g:
            body(g, 1)
            body(g + 1, 0)
        body(NG - 1, 1)
        last(NG - 1, 1)

    with nc.Block() as block:
        @block.sync
        def _(sp):
            def load(g, u):
                Apart.wait(sp, r_w, 32 * g)
                later(sp, r_y, g - 1)
                cols = slice(GE * g, GE * g + GE) if isinstance(g, int) else bass.ds(g * GE, GE)
                sp.dma_start(t.w13[:, u, :, :], d.w13T[:, cols, :]).then_inc(r_w, 16)
                sp.dma_start(t.w2[:, u, :, :], d.w2T[:, cols, :]).then_inc(r_w, 16)
                later(sp, r_x, 16 * g)
                later(sp, r_T, g - 1)
                pl = d.places.rearrange("(g k p) w -> g p k w", p=128, k=4)
                src = pl[g] if isinstance(g, int) else pl[bass.ds(g, 1)].rearrange("o p k w -> (o p) k w")
                sp.dma_start(t.xp[:, u, :, :], src[:, :, 0:D]).then_inc(r_x, 16)

            def store(g, u):
                Apart.wait(sp, r_yo, g + 1)
                later(sp, r_out, 16 * g)
                pl = d.yplaces.rearrange("(g k p) w -> g p k w", p=128, k=4)
                dst = pl[g] if isinstance(g, int) else pl[bass.ds(g, 1)].rearrange("o p k w -> (o p) k w")
                sp.dma_start(dst, t.yo[:, u, :, :]).then_inc(r_out, 16)

            def body(g, u):
                load(g, u)
                if not isinstance(g, int) or g >= 1:
                    store(g - 1, 1 - u)

            for half in range(2):
                src = bass.AP(tensor=d.places.tensor, offset=D + half * (CAP * PAY0 + 1),
                              ap=[[PAY0, CAP], [2 * (CAP * PAY0 + 1), E0 // 2]])
                sp.dma_start(t.wt[CAP * half:CAP * half + CAP, :], src,
                             allow_slow_non_contiguous=True).then_inc(r_wt, 16)
            groups(sp, body, store)
            sp.wait_ge(r_out, 16 * NG)

        @block.tensor
        def _(pe):
            def hidden(b, c):
                later(pe, s_u, 2 * b + c - 1)
                rhs = t.XT[:, T4 * b:T4 * b + T4, :] if isinstance(b, int) else t.XT[:, bass.ds(b * T4, T4), :]
                for k, bank in ((0, H1[c]), (1, H3[c])):
                    mm = nc.tensor.matmul(bank[0:I0, :], t.ws13T[:, (2 * k + c) * I0:(2 * k + c + 1) * I0],
                                          rhs.rearrange("p k q -> p (k q)"), start=True, stop=True)
                mm.then_inc(s_h, 1)

            def project(b):
                later(pe, s_zadd, b)
                pe.wait_ge(s_u, 2 * b + 2)
                for k in range(T4):
                    for c in range(2):
                        mm = nc.tensor.matmul(ps[4][:, D * k:D * k + D], t.uT[:, c, S * k:S * k + S],
                                              t.ws2T[:, c, :], start=(c == 0), stop=(c == 1))
                mm.then_inc(s_z, 1)

            hidden(0, 0)
            hidden(0, 1)

            def block4(b):
                hidden(b + 1, 0)
                project(b)
                hidden(b + 1, 1)

            block4(0)
            with pe.Fori(1, NB - 1) as b:
                block4(b)
            project(NB - 1)

            def places(g, u):
                pe.wait_ge(r_x, 16 * (g + 1))
                later(pe, r_Tc, g)
                for k in range(4):
                    mm = nc.tensor.transpose(TP[:, 128 * k:128 * k + 128], t.xp[:, u, k, :], t.ident[:])
                mm.then_inc(r_T, 1)
                pe.wait_ge(r_Tc, g + 1)
                pe.wait_ge(r_w, 32 * (g + 1))
                later(pe, r_u, g - 1)
                if isinstance(g, int) and g < 2:
                    pe.wait_ge(s_u, 2 * NB)
                for e in range(GE):
                    for k, bank in ((0, H1[u]), (1, H3[u])):
                        mm = nc.tensor.matmul(bank[0:I0, CAP * e:CAP * e + CAP], t.w13[:, u, e, k * I0:(k + 1) * I0],
                                              t.xpT[:, u, CAP * e:CAP * e + CAP], start=True, stop=True)
                mm.then_inc(r_h, 1)

            def outputs(g, u):
                pe.wait_ge(r_u, g + 1)
                later(pe, r_yo, g - 1)
                if isinstance(g, int) and g == 0:
                    pe.wait_ge(s_zadd, NB)
                for e in range(GE):
                    h = CAP * (e % 2)
                    mm = nc.tensor.matmul(Y[u][h:h + CAP, D * (e // 2):D * (e // 2) + D],
                                          t.gT[:, u, CAP * e:CAP * e + CAP], t.w2[:, u, e, :], start=True, stop=True)
                mm.then_inc(r_y, 1)

            def body(g, u):
                places(g, u)
                if not isinstance(g, int) or g >= 1:
                    outputs(g - 1, 1 - u)

            groups(pe, body, outputs)

        @block.scalar
        def _(act):
            def block4(b):
                for c in range(2):
                    act.wait_ge(s_h, 2 * b + c + 1)
                    later(act, s_u, 2 * b + c)
                    nc.scalar.activation(t.em[:], H1[c][0:I0, :], ACT.Exp, scale=-1.0).then_inc(s_e, 1)

            block4(0)
            with act.Fori(1, NB) as b:
                block4(b)

            def body(g, u):
                act.wait_ge(r_T, g + 1)
                later(act, r_h, g - 1)
                nc.scalar.activation(t.xpT[:, u, :], TP[:, :], ACT.Copy).then_inc(r_Tc, 1)
                act.wait_ge(r_h, g + 1)
                later(act, r_u, g)
                nc.scalar.activation(t.em[:], H1[u][0:I0, :], ACT.Exp, scale=-1.0).then_inc(r_e, 1)

            act.wait_ge(s_u, 2 * NB)
            groups(act, body, lambda g, u: None)

        @block.vector
        def _(dve):
            def block4(b):
                c_ = Steps(dve, s_vs, 6, b)
                for c in range(2):
                    dve.wait_ge(s_e, 2 * b + c + 1)
                    if c == 0:
                        later(dve, s_z, b)
                    silu_gate(nc, dve, c_, t.em[:], t.er[:], t.uT[:, c, :], H1[c][0:I0, :],
                              H3[c][0:I0, :]).then_inc(s_u, 1)
                dve.wait_ge(s_z, b + 1)
                tiles = slice(0, T4) if isinstance(b, int) else bass.ds(b * T4, T4)
                rows = t.X[:, tiles, :].rearrange("p k d -> p (k d)")
                nc.vector.scalar_tensor_tensor(rows, ps[4][:, :], t.gate[:, 1:2], rows, ALU.mult,
                                               ALU.add).then_inc(s_zadd, 1)

            block4(0)
            with dve.Fori(1, NB) as b:
                block4(b)

            def scale(g, u):
                dve.wait_ge(r_y, g + 1)
                later(dve, r_out, 16 * (g - 1))
                w = t.wt[:, 4 * g:4 * g + 4] if isinstance(g, int) else t.wt[:, bass.ds(g * 4, 4)]
                nc.vector.tensor_tensor(t.yo[:, u, :, :], Y[u][:, :].rearrange("p (k d) -> p k d", k=4),
                                        w.unsqueeze(2).broadcast_to([128, 4, D]), ALU.mult).then_inc(r_yo, 1)

            def body(g, u):
                c_ = Steps(dve, r_vs, 3, g)
                dve.wait_ge(r_e, g + 1)
                later(dve, r_y, g - 1)
                silu_gate(nc, dve, c_, t.em[:], t.er[:], t.gT[:, u, :], H1[u][0:I0, :],
                          H3[u][0:I0, :]).then_inc(r_u, 1)
                if isinstance(g, int) and g == 0:
                    return
                scale(g - 1, 1 - u)

            dve.wait_ge(r_wt, 32)
            groups(dve, body, scale)


def choice_block(nc, t, d, sem, ps):
    turned, copied, vstep, summed, k_v, k_cnt, k_sum = (sem(f"choice_{x}") for x in (
        "scores_T", "scores_T_copied", "vector_step", "sums", "bit_step", "bit_counts", "bit_sums"))
    BITS = 30
    with nc.Block() as block:
        @block.tensor
        def _(pe):
            for h in range(2):
                mm = nc.tensor.transpose(ps[0][:, 128 * h:128 * h + 128],
                                         t.scores1[:, 4 * h:4 * h + 4, :].rearrange("p e k -> p (e k)"), t.ident[:])
            mm.then_inc(turned, 1)
            with pe.Fori(0, BITS) as k:
                pe.wait_ge(k_cnt, 2 * (k + 1))
                nc.tensor.matmul(ps[1][:, 0:2], t.same[:], t.cnt[:], start=True, stop=True).then_inc(k_sum, 1)
            for n, (weights, counts) in enumerate(((t.same, t.cnt), (t.earlier, t.cnt2), (t.earlier, t.cnt3))):
                pe.wait_ge(copied, n + 2)
                nc.tensor.matmul(ps[2 + n][:, 0:2], weights[:], counts[:], start=True, stop=True).then_inc(summed, 1)

        @block.vector
        def _(dve):
            ve = nc.vector
            c = Steps(dve, vstep, 0, 0)
            dve.wait_ge(turned, 1)
            ve.tensor_copy(t.sT[:], ps[0][:, 0:256].rearrange("p (h q) -> p h q", h=2)).then_inc(copied, 1)
            dve.wait_ge(copied, 1)
            c.then(ve.memset(t.thr[:], 0))
            c.then(ve.memset(t.bitf[:], float(2 ** (BITS - 1))))
            c.then(ve.tensor_copy(t.cand[:], t.bitf[:]))
            with dve.Fori(0, BITS) as k:
                s = Steps(dve, k_v, 5, k)
                for h in range(2):
                    ve.tensor_scalar(t.junk[:, h, :], t.sT[:, h, :], t.cand[:, h:h + 1].bitcast(F32), 0.0,
                                     ALU.is_ge, ALU.add, accum_out=t.cnt[:, h:h + 1]).then_inc(k_cnt, 1)
                dve.wait_ge(k_cnt, 2 * (k + 1))
                dve.wait_ge(k_sum, k + 1)
                s.then(ve.scalar_tensor_tensor(t.bitu[:], ps[1][:, 0:2], float(K1), t.bitf[:], ALU.is_ge, ALU.mult))
                s.then(ve.tensor_scalar(t.bitf[:], t.bitf[:], 0.5, None, ALU.mult))
                s.then(ve.tensor_tensor(t.thr[:], t.thr[:], t.bitu[:], ALU.bitwise_or))
                s.then(ve.tensor_copy(t.cand[:], t.bitf[:]))
                s.then(ve.tensor_tensor(t.cand[:], t.cand[:], t.thr[:], ALU.bitwise_or))
            for h in range(2):
                thr = t.thr[:, h:h + 1].bitcast(F32)
                c.then(ve.tensor_scalar(t.gt[:, h, :], t.sT[:, h, :], thr, 0.0, ALU.is_gt, ALU.add,
                                        accum_out=t.cnt[:, h:h + 1]))
                c.then(ve.tensor_scalar(t.eq[:, h, :], t.sT[:, h, :], thr, 0.0, ALU.is_equal, ALU.add,
                                        accum_out=t.cnt2[:, h:h + 1]))
                c.then(ve.tensor_tensor_scan(t.cum[:, h, :], t.eq[:, h, :], t.eq[:, h, :], 0.0, ALU.add, ALU.max))
            ve.memset(t.junk[:, 0, 0:1], 0.0).then_inc(copied, 1)
            ve.memset(t.junk[:, 0, 1:2], 0.0).then_inc(copied, 1)
            dve.wait_ge(summed, 2)
            c.then(ve.tensor_scalar(t.left[:], ps[2][:, 0:2], -1.0, float(K1), ALU.mult, ALU.add))
            c.then(ve.tensor_tensor(t.left[:], t.left[:], ps[3][:, 0:2], ALU.subtract))
            for h in range(2):
                c.then(ve.scalar_tensor_tensor(t.eq[:, h, :], t.cum[:, h, :], t.left[:, h:h + 1], t.eq[:, h, :],
                                               ALU.is_le, ALU.mult))
                c.then(ve.tensor_tensor(t.gt[:, h, :], t.gt[:, h, :], t.eq[:, h, :], ALU.add))
                c.then(ve.tensor_tensor_scan(t.cum[:, h, :], t.gt[:, h, :], t.gt[:, h, :], 0.0, ALU.add, ALU.max))
                c.then(ve.tensor_copy(t.cnt3[:, h:h + 1], t.cum[:, h, 127:128]))
            ve.memset(t.junk[:, 0, 0:1], 0.0).then_inc(copied, 1)
            dve.wait_ge(summed, 3)
            c.then(ve.tensor_copy(t.first[:], ps[4][:, 0:2]))
            c.then(ve.tensor_tensor(t.last[:], t.first[:], t.cnt3[:], ALU.add))
            c.then(ve.memset(t.firsts[:], float(N)))
            c.then(ve.memset(t.lasts[:], 0.0))
            for e in range(E1):
                j, h = 32 * (e % 4), e // 4
                c.then(ve.tensor_copy(t.firsts[j:j + 32, e:e + 1], t.first[j:j + 32, h:h + 1]))
                c.then(ve.tensor_copy(t.lasts[j:j + 32, e:e + 1], t.last[j:j + 32, h:h + 1]))
                c.then(ve.tensor_scalar(t.counts[:, e, 0:128], t.cum[:, h, :], t.first[:, h:h + 1], None, ALU.add))
                c.then(ve.tensor_copy(t.counts[:, e, 128:129], t.tile_start[:]))


def experts1_block(nc, t, d, sem, ps):
    NT = K1 // 128
    C1 = I1 // 128
    ev = Named()
    ev.range = sem("moe_range")
    ev.oh = sem("moe_oh")
    ev.counted = sem("moe_counted")
    ev.picked = sem("moe_picked")
    ev.listed = sem("moe_listed")
    ev.gathered = sem("moe_gathered")
    ev.turned = sem("moe_turned")
    ev.turned_copied = sem("moe_turned_copied")
    ev.hidden = sem("moe_hidden")
    ev.gelu = sem("moe_gelu")
    ev.out = sem("moe_out")
    ev.scaled = sem("moe_scaled")
    ev.added = sem("moe_added")
    ev.weights = sem("moe_weights")
    ev.v_range = sem("moe_v_range")
    ev.v_y = sem("moe_v_y")
    ev.gate_ready = sem("moe_gate_ready")
    HB, Y, TB = ps[0:4], ps[4:6], ps[6:8]

    def later(eng, event, value):
        if not isinstance(value, int) or value > 0:
            eng.wait_ge(event, value)

    def experts(eng, ahead, body):
        ahead(0, 0)
        body(0, 0)
        body(1, 1)
        with eng.Fori(2, E1 - 3, 2) as e:
            body(e, 0)
            body(e + 1, 1)
        body(E1 - 2, 0)
        body(E1 - 1, 1)

    def last(e):
        return isinstance(e, int) and e == E1 - 1

    with nc.Block() as block:
        @block.sync
        def _(sp):
            def load(e, u):
                Apart.wait(sp, ev.weights, 64 * e)
                later(sp, ev.scaled, 2 * (e - 1))
                sp.dma_start(t.w1x[:, u, :], row(d.w1x, e)).then_inc(ev.weights, 16)
                sp.dma_start(t.w2x[:, u, :, :].rearrange("p c d -> p (c d)"), row(d.w2x, e)).then_inc(ev.weights, 16)
                b1 = d.b1x[e] if isinstance(e, int) else d.b1x[bass.ds(e, 1)].rearrange("o p c -> (o p) c")
                sp.dma_start(t.b1x[:, u, :], b1).then_inc(ev.weights, 16)
                b2 = d.b2x[e:e + 1, :] if isinstance(e, int) else d.b2x[bass.ds(e, 1), :]
                sp.dma_start(t.b2x[:, u, :], b2.rearrange("o d -> (o d)").partition_broadcast(128)
                             ).then_inc(ev.weights, 16)

            def body(e, u):
                if not last(e):
                    load(e + 1, 1 - u)

            experts(sp, load, body)

        @block.tensor
        def _(pe):
            def pick(e, u):
                pe.wait_ge(ev.oh, e + 1)
                for k in range(NT):
                    later(pe, ev.counted, NT * e + k - 1)
                    if k < 2:
                        later(pe, ev.turned_copied, 2 * e)
                    rhs = t.counts[:, e, :] if isinstance(e, int) else \
                        t.counts[:, bass.ds(e, 1), :].rearrange("p o w -> p (o w)")
                    nc.tensor.matmul(TB[k % 2][:, 0:129], t.oh[:, 128 * k:128 * k + 128], rhs,
                                     start=True, stop=True).then_inc(ev.picked, 1)

            def turn(e, u):
                pe.wait_ge(ev.gathered, 16 * NT * (e + 1))
                for s in range(2):
                    pe.wait_ge(ev.counted, NT * (e + 1))
                    for k in range(4):
                        mm = nc.tensor.transpose(TB[s][:, 128 * k:128 * k + 128], t.xg[:, u, 4 * s + k, 0:D], t.ident[:])
                    mm.then_inc(ev.turned, 1)

            def hidden(e, u, s):
                if s == 0:
                    pe.wait_ge(ev.weights, 64 * (e + 1))
                pe.wait_ge(ev.turned_copied, 2 * e + s + 1)
                for c in range(C1):
                    later(pe, ev.gelu, 8 * e + 4 * s + c - 3)
                    nc.tensor.matmul(HB[c][:, :], t.w1x[:, u, 128 * c:128 * c + 128],
                                     t.xgT[:, u, 512 * s:512 * s + 512], start=True, stop=True).then_inc(ev.hidden, 1)

            def out(e, u, s):
                pe.wait_ge(ev.gelu, 8 * e + 4 * s + 4)
                later(pe, ev.scaled, 2 * e + s - 1)
                for k in range(4):
                    for c in range(C1):
                        mm = nc.tensor.matmul(Y[s][:, D * k:D * k + D], t.ge[:, s, c, 128 * k:128 * k + 128],
                                              t.w2x[:, u, c, :], start=(c == 0), stop=(c == C1 - 1))
                mm.then_inc(ev.out, 1)

            def ahead(e, u):
                pick(e, u)
                turn(e, u)

            def body(e, u):
                hidden(e, u, 0)
                if not last(e):
                    pick(e + 1, 1 - u)
                hidden(e, u, 1)
                out(e, u, 0)
                if not last(e):
                    turn(e + 1, 1 - u)
                out(e, u, 1)

            experts(pe, ahead, body)

        @block.scalar
        def _(act):
            def copy(e, u):
                for s in range(2):
                    act.wait_ge(ev.turned, 2 * e + s + 1)
                    later(act, ev.hidden, 8 * (e - 1))
                    nc.scalar.activation(t.xgT[:, u, 512 * s:512 * s + 512], TB[s][:, :],
                                         ACT.Copy).then_inc(ev.turned_copied, 1)

            def gelu(e, u, s):
                for c in range(C1):
                    act.wait_ge(ev.hidden, 8 * e + 4 * s + c + 1)
                    later(act, ev.out, 2 * e + s - 1)
                    nc.scalar.activation(t.ge[:, s, c, :], HB[c][:, :], ACT.Gelu,
                                         bias=t.b1x[:, u, c:c + 1]).then_inc(ev.gelu, 1)

            def body(e, u):
                gelu(e, u, 0)
                gelu(e, u, 1)
                if not last(e):
                    copy(e + 1, 1 - u)

            experts(act, copy, body)

        @block.gpsimd
        def _(pool):
            def gather(e, u):
                pool.wait_ge(ev.listed, e + 1)
                later(pool, ev.gathered, 16 * NT * e)
                Apart.wait(pool, ev.turned, 2 * (e - 1))
                Apart.wait(pool, ev.gate_ready, e - 1)
                for k in range(NT):
                    nc.gpsimd.indirect_dma_start(
                        out=t.xg[:, u, k, :], out_offset=None, in_=d.rows_flat,
                        in_offset=bass.IndirectOffsetOnAxis(ap=t.token[:, u, k:k + 1], axis=0),
                        ).then_inc(ev.gathered, 16)

            def add(e, u):
                later(pool, ev.added, 16 * NT * e)
                for k in range(NT):
                    if k % 4 == 0:
                        Apart.wait(pool, ev.scaled, 2 * e + k // 4 + 1)
                    nc.gpsimd.indirect_dma_start(
                        out=d.out_flat, out_offset=bass.IndirectOffsetOnAxis(ap=t.token[:, u, k:k + 1], axis=0),
                        in_=t.y1[:, u, k, :], in_offset=None, compute_op=ALU.add).then_inc(ev.added, 16)

            def body(e, u):
                if not last(e):
                    gather(e + 1, 1 - u)
                add(e, u)

            experts(pool, gather, body)
            pool.wait_ge(ev.added, 16 * NT * E1)

        @block.vector
        def _(dve):
            ve = nc.vector

            def ranges(e, u):
                s = Steps(dve, ev.v_range, 1, e)
                later(dve, ev.picked, NT * e)
                col = (lambda x: x[:, e:e + 1]) if isinstance(e, int) else (lambda x: x[:, bass.ds(e, 1)])
                s.then(ve.tensor_scalar(t.oh[:], t.slotno[:], col(t.firsts), None, ALU.is_ge))
                ve.scalar_tensor_tensor(t.oh[:], t.slotno[:], col(t.lasts), t.oh[:], ALU.is_lt,
                                        ALU.mult).then_inc(ev.oh, 1)

            def count(e, u):
                for k in range(NT):
                    dve.wait_ge(ev.picked, NT * e + k + 1)
                    ve.tensor_scalar(t.junk2[:, k % 2, :], TB[k % 2][:, 0:128], t.rank[:, k:k + 1],
                                     TB[k % 2][:, 128:129], ALU.is_le, ALU.add,
                                     accum_out=t.tokf[:, u, k:k + 1]).then_inc(ev.counted, 1)
                dve.wait_ge(ev.counted, NT * (e + 1))
                later(dve, ev.added, 16 * NT * (e - 1))
                ve.tensor_copy(t.token[:, u, :], t.tokf[:, u, :]).then_inc(ev.listed, 1)

            def gates(e, u):
                dve.wait_ge(ev.gathered, 16 * NT * (e + 1))
                col = slice(D + e, D + e + 1) if isinstance(e, int) else bass.ds(e + D, 1)
                ve.tensor_scalar(t.gs[:, u, :], t.xg[:, u, :, col].rearrange("p k o -> p (k o)"), t.gate[:, 3:4],
                                 None, ALU.mult).then_inc(ev.gate_ready, 1)
                dve.wait_ge(ev.gate_ready, e + 1)

            def scale(e, u, s):
                st = Steps(dve, ev.v_y, 2, e)
                st.k = s
                dve.wait_ge(ev.out, 2 * e + s + 1)
                later(dve, ev.added, 16 * NT * (e - 1))
                y = t.y1[:, u, 4 * s:4 * s + 4, :]
                st.then(ve.tensor_tensor(y, Y[s][:, :].rearrange("p (k d) -> p k d", k=4),
                                         t.b2x[:, u, :].unsqueeze(1).broadcast_to([128, 4, D]), ALU.add))
                ve.tensor_tensor(y, y, t.gs[:, u, 4 * s:4 * s + 4].unsqueeze(2).broadcast_to([128, 4, D]),
                                 ALU.mult).then_inc(ev.scaled, 1)

            def ahead(e, u):
                ranges(e, u)
                count(e, u)

            def body(e, u):
                if not last(e):
                    ranges(e + 1, 1 - u)
                    count(e + 1, 1 - u)
                gates(e, u)
                scale(e, u, 0)
                scale(e, u, 1)

            experts(dve, ahead, body)


def flamingo_kernel(nc, **dram):
    d = Named()
    d.x = dram["x"]
    d.ctxT = dram["ctxT"]
    d.fside = dram["fside"]
    d.mask0 = dram["mask0"]
    d.pad = dram["pad"]
    d.padT = dram["padT"]
    d.graw = dram["graw"]
    d.wqT0 = dram["wqT0"]
    d.wkT0 = dram["wkT0"]
    d.wvT0 = dram["wvT0"]
    d.woT0 = dram["woT0"]
    d.wqT1 = dram["wqT1"]
    d.wkT1 = dram["wkT1"]
    d.wvT1 = dram["wvT1"]
    d.woT1 = dram["woT1"]
    d.qkvb = dram["qkvb"]
    d.outb = dram["outb"]
    d.hs = dram["hs"]
    d.gateT = dram["gateT"]
    d.gb = dram["gb"]
    d.wrT = dram["wrT"]
    d.ws13T = dram["ws13T"]
    d.ws2T = dram["ws2T"]
    d.w13T = dram["w13T"]
    d.w2T = dram["w2T"]
    d.w1x = dram["w1x"]
    d.w2x = dram["w2x"]
    d.b1x = dram["b1x"]
    d.b2x = dram["b2x"]
    d.out = dram["out"]
    d.scrq = nc.dram_tensor("query_stack", [BLOCKS * D, S], BF16, kind="Internal").ap()
    d.scrk = nc.dram_tensor("key_stack", [BLOCKS * D, KV], BF16, kind="Internal").ap()
    d.places = nc.dram_tensor("places", [E0 * CAP, PAY0], F32, kind="Internal").ap()
    d.yplaces = nc.dram_tensor("places_out", [E0 * CAP, D], F32, kind="Internal").ap()
    d.rows = nc.dram_tensor("token_rows", [B, S, PAY1], F32, kind="Internal").ap()
    d.rows_flat = d.rows.rearrange("b s w -> (b s) w")
    d.out_flat = d.out.rearrange("b s w -> (b s) w")

    with ExitStack() as ctx:
        def sem(name):
            return ctx.enter_context(nc.semaphore(name))

        t = Named()
        Apart.set_up = sem("set_up")

        def tile(where, name, shape, dt, partitions=128):
            return where.enter_context(nc.sbuf_tensor(name, [partitions] + shape, dt))

        t.X = tile(ctx, "X", [B, D], F32)
        t.gate = tile(ctx, "gate", [4], F32)
        t.graw = tile(ctx, "graw", [4], F32)
        t.ident = tile(ctx, "ident", [128], F32)
        t.identb = tile(ctx, "identb", [128], BF16)
        t.scores1 = tile(ctx, "scores1", [E1, B], F32)
        t.slots = tile(ctx, "slots", [B, 8], U32)
        t.minus_half = tile(ctx, "minus_half", [1], F32)
        t.XT = tile(ctx, "XT", [B, D], F32)
        t.tile_start = tile(ctx, "tile_start", [1], F32)
        t.rank = tile(ctx, "rank", [K1 // 128], F32)
        t.slotno = tile(ctx, "slotno", [K1], F32)
        t.same = tile(ctx, "same", [128], F32)
        t.earlier = tile(ctx, "earlier", [128], F32)
        ps = [ctx.enter_context(nc.psum_tensor(f"bank{k}", [128, 512], F32)) for k in range(8)]
        with ExitStack() as ex0:
            t.ws13T = tile(ex0, "ws13T", [4 * I0], F32)
            t.gateT = tile(ex0, "gateT", [E0], F32)
            t.wrT = tile(ex0, "wrT", [E1], F32)
            t.em = tile(ex0, "em", [512], F32, I0)
            t.er = tile(ex0, "er", [512], F32, I0)
            t.uT = tile(ex0, "uT", [2, 512], F32, I0)
            t.gT = tile(ex0, "gT", [2, 512], F32, I0)
            t.ws2T = tile(ex0, "ws2T", [2, D], F32, I0)
            t.w13 = tile(ex0, "w13", [2, 8, 2 * I0], F32)
            t.w2 = tile(ex0, "w2", [2, 8, D], F32, I0)
            t.xp = tile(ex0, "xp", [2, 4, D], F32)
            t.xpT = tile(ex0, "xpT", [2, 512], F32)
            t.yo = tile(ex0, "yo", [2, 4, D], F32)
            t.wt = tile(ex0, "wt", [E0 // 2], F32)
            t.qkvb = tile(ex0, "qkvb", [3], F32)
            t.hs = tile(ex0, "hs", [1], F32)
            t.outb = tile(ex0, "outb", [D], F32)
            t.outbg = tile(ex0, "outbg", [D], F32)
            t.gb = tile(ex0, "gb", [E0], F32)
            t.mask_u8 = tile(ex0, "mask_u8", [KV], U8)
            t.mask_f = tile(ex0, "mask_f", [KV], F32)
            t.mask0 = tile(ex0, "mask0", [KV], BF16)
            t.rowany = tile(ex0, "rowany", [1], F32)
            t.pad_u8 = tile(ex0, "pad_u8", [B * KV], U8)
            t.padfar = tile(ex0, "padfar", [B * KV], F32)
            t.padT_u8 = tile(ex0, "padT_u8", [B], U8, KV)
            t.padinf = tile(ex0, "padinf", [B], F32, KV)
            t.qbs = tile(ex0, "qbs", [1], F32)
            t.zeros = tile(ex0, "zeros", [8 * PAY0], F32)
            t.before = tile(ex0, "before", [128], BF16)
            t.onesb = tile(ex0, "onesb", [128], BF16)
            t.pick = tile(ex0, "pick", [H, KV], BF16)
            t.headcols = tile(ex0, "headcols", [G, 32], F32)
            t.iota_e = tile(ex0, "iota_e", [E0], I32)
            t.lastplace = tile(ex0, "lastplace", [E0], F32)
            t.iota_r = tile(ex0, "iota_r", [K1 // 128], I32)
            t.iota_s = tile(ex0, "iota_s", [K1], I32)
            t.iota_t = tile(ex0, "iota_t", [1], I32)
            t.ctx = tile(ex0, "ctx", [2, KV], F32)
            t.fb = tile(ex0, "fb", [2, KV], F32)
            t.fb2 = tile(ex0, "fb2", [2, KV], F32)
            t.bp = tile(ex0, "bp", [2, 3, KV], BF16)
            t.qkf = tile(ex0, "qkf", [2, QK], F32)
            t.parts = tile(ex0, "parts", [2, 3, QK], BF16)
            t.rest = tile(ex0, "rest", [QK], F32)
            t.Qs = tile(ex0, "Qs", [2, H, S], BF16)
            t.Ks = tile(ex0, "Ks", [2, H, KV], BF16)
            t.Vb = tile(ex0, "Vb", [2, G, 160], F32)
            t.xn = tile(ex0, "xn", [2, D], F32)
            t.xnT = tile(ex0, "xnT", [2, D], F32)
            t.st = tile(ex0, "st", [2, 6], F32)
            t.mv = tile(ex0, "mv", [2, 2, 2], F32)
            t.rs = tile(ex0, "rs", [2, 2, 1], F32)
            t.rstd = tile(ex0, "rstd", [2, 2, 1], F32)
            t.mx = tile(ex0, "mx", [H], F32)
            t.nm = tile(ex0, "nm", [2, 48], BF16)
            t.nmT = tile(ex0, "nmT", [2, S], BF16)
            t.PT = tile(ex0, "PT", [G, 512], F32)
            t.rsum = tile(ex0, "rsum", [S], F32)
            t.oT = tile(ex0, "oT", [2, S], F32)
            t.payload = tile(ex0, "payload", [2, PAY0], F32)
            t.xT2 = tile(ex0, "xT2", [2, D], F32)
            t.lmax = tile(ex0, "lmax", [1], F32)
            t.negmax = tile(ex0, "negmax", [2, 1], F32)
            t.ex = tile(ex0, "ex", [2, E0], F32)
            t.exsum = tile(ex0, "exsum", [2, 1], F32)
            t.exrec = tile(ex0, "exrec", [1], F32)
            t.biased = tile(ex0, "biased", [E0], F32)
            t.top8 = tile(ex0, "top8", [8], F32)
            t.above = tile(ex0, "above", [E0], F32)
            t.n_above = tile(ex0, "n_above", [1], F32)
            t.equal = tile(ex0, "equal", [E0], F32)
            t.n_equal = tile(ex0, "n_equal", [E0], F32)
            t.wanted = tile(ex0, "wanted", [1], F32)
            t.sel = tile(ex0, "sel", [2, E0], BF16)
            t.sacc = tile(ex0, "sacc", [2, E0], BF16)
            t.fits = tile(ex0, "fits", [E0], F32)
            t.back = tile(ex0, "back", [E0], F32)
            t.top8b = tile(ex0, "top8b", [8], F32)
            t.slot = tile(ex0, "slot", [2, 8], U32)
            t.slotg = tile(ex0, "slotg", [2, 8], U32)
            t.yrows = tile(ex0, "yrows", [2, K0, D], F32)
            t.ysum = tile(ex0, "ysum", [D], F32)
            t.wqT = [tile(ex0, f"wqT{L}", [D], F32) for L in range(2)]
            t.wkT = [tile(ex0, f"wkT{L}", [D], F32) for L in range(2)]
            t.wvT = [tile(ex0, f"wvT{L}", [D], F32) for L in range(2)]
            t.woT = [tile(ex0, f"woT{L}", [D], F32) for L in range(2)]
            t.padfar_rows = t.padfar[:].rearrange("p (b k) -> p b k", b=B)
            setup_block(nc, t, d, sem, ps)
            attention_block(nc, 0, t, d, sem, ps)
            experts0_block(nc, t, d, sem, ps)
            attention_block(nc, 1, t, d, sem, ps)
        with ExitStack() as ex1:
            t.sT = tile(ex1, "sT", [2, 128], F32)
            t.thr = tile(ex1, "thr", [2], U32)
            t.bitf = tile(ex1, "bitf", [2], F32)
            t.bitu = tile(ex1, "bitu", [2], U32)
            t.cand = tile(ex1, "cand", [2], U32)
            t.junk = tile(ex1, "junk", [2, 128], F32)
            t.cnt = tile(ex1, "cnt", [2], F32)
            t.cnt2 = tile(ex1, "cnt2", [2], F32)
            t.cnt3 = tile(ex1, "cnt3", [2], F32)
            t.gt = tile(ex1, "gt", [2, 128], F32)
            t.eq = tile(ex1, "eq", [2, 128], F32)
            t.cum = tile(ex1, "cum", [2, 128], F32)
            t.left = tile(ex1, "left", [2], F32)
            t.first = tile(ex1, "first", [2], F32)
            t.last = tile(ex1, "last", [2], F32)
            t.firsts = tile(ex1, "firsts", [E1], F32)
            t.lasts = tile(ex1, "lasts", [E1], F32)
            t.counts = tile(ex1, "counts", [E1, 129], F32)
            t.oh = tile(ex1, "oh", [K1], F32)
            t.junk2 = tile(ex1, "junk2", [2, 128], F32)
            t.tokf = tile(ex1, "tokf", [2, 8], F32)
            t.token = tile(ex1, "token", [2, 8], U32)
            t.xg = tile(ex1, "xg", [2, 8, PAY1], F32)
            t.xgT = tile(ex1, "xgT", [2, K1], F32)
            t.ge = tile(ex1, "ge", [2, 4, 512], F32)
            t.y1 = tile(ex1, "y1", [2, 8, D], F32)
            t.gs = tile(ex1, "gs", [2, 8], F32)
            t.w1x = tile(ex1, "w1x", [2, I1], F32)
            t.w2x = tile(ex1, "w2x", [2, 4, D], F32)
            t.b1x = tile(ex1, "b1x", [2, 4], F32)
            t.b2x = tile(ex1, "b2x", [2, D], F32)
            choice_block(nc, t, d, sem, ps)
            experts1_block(nc, t, d, sem, ps)




def laid_out(i):
    import numpy as np

    def head_last(w):
        return w.reshape(w.shape[0], H, DK).transpose(0, 2, 1).reshape(w.shape[0], D)

    inw, inb = i["L1_xattn_in_proj_weight"], i["L1_xattn_in_proj_bias"]
    qb, kb, vb = inb.reshape(3, D)
    perm = lambda v: v.reshape(H, DK).T.reshape(D)
    a = {
        "x": i["x"],
        "ctxT": i["ctx_1024"].transpose(0, 2, 1),
        "fside": i["fside_BxSxS2_0"],
        "mask0": i["mask_1x1xSxS2_bk0"].reshape(S, KV),
        "pad": i["mask_BxS2_bf0"].reshape(B * KV),
        "padT": np.ascontiguousarray(i["mask_BxS2_bf0"].T),
        "graw": np.stack([i["g_xattn"][0], i["g_ffn"][0], i["g_xattn"][1], i["g_ffn"][1]]),
        "wqT0": head_last(i["L0_xattn_w_q"].T), "wkT0": head_last(i["L0_xattn_w_k"].T),
        "wvT0": i["L0_xattn_w_v"].T, "woT0": i["L0_xattn_w_o"].T,
        "wqT1": head_last(inw[0:D].T), "wkT1": head_last(inw[D:2 * D].T),
        "wvT1": inw[2 * D:].T, "woT1": i["L1_xattn_out_w"].T,
        "qkvb": np.stack([perm(qb), perm(kb), vb], axis=1), "outb": i["L1_xattn_out_b"],
        "hs": np.repeat(i["L1_xattn_head_scales"], DK)[:, None],
        "gateT": i["L0_ffn_gate_w"].T, "gb": i["L0_ffn_gate_b"], "wrT": i["L1_ffn_Wr"],
        "ws13T": np.concatenate([i["L0_ffn_ws1"].T, i["L0_ffn_ws3"].T], axis=1),
        "ws2T": i["L0_ffn_ws2"].T.reshape(2, I0, D).transpose(1, 0, 2),
        "w13T": np.concatenate([i["L0_ffn_w1"], i["L0_ffn_w3"]], axis=1).transpose(2, 0, 1),
        "w2T": i["L0_ffn_w2"].transpose(2, 0, 1),
        "w1x": i["L1_ffn_W1"],
        "w2x": i["L1_ffn_W2"].reshape(E1, 4, 128, D).transpose(0, 2, 1, 3).reshape(E1, 128, 4 * D),
        "b1x": i["L1_ffn_b1"].reshape(E1, 4, 128).transpose(0, 2, 1), "b2x": i["L1_ffn_b2"],
    }
    return {k: np.ascontiguousarray(v) for k, v in a.items()}


def kernel(**inputs):
    import numpy as _np
    import concourse.bacc as _bacc
    from concourse import mybir as _mybir
    from concourse.bass_utils import run_bass_kernel_spmd as _run

    nc = _bacc.Bacc("TRN2", target_bir_lowering=False, num_devices=1)
    arrays = laid_out({k: _np.asarray(v) for k, v in inputs.items()})
    args = {k: nc.dram_tensor(f"in_{k}", a.shape, _mybir.dt.from_np(a.dtype), kind="ExternalInput").ap()
            for k, a in arrays.items()}
    args["out"] = nc.dram_tensor("out_0", (B, S, D), _mybir.dt.float32, kind="ExternalOutput").ap()
    flamingo_kernel(nc, **args)
    r = _run(nc, [{f"in_{k}": a for k, a in arrays.items()}], core_ids=[0])
    return r.results[0]["out_0"]
```

```python
from contextlib import ExitStack

import concourse.bass as bass
from concourse import mybir

F32 = mybir.dt.float32
BF16 = mybir.dt.bfloat16
U32 = mybir.dt.uint32
I32 = mybir.dt.int32
U8 = mybir.dt.uint8
ALU = mybir.AluOpType
ACT = mybir.ActivationFunctionType
AX = mybir.AxisListType

B, S, D = 32, 128, 128
KV = 120
H, DK = 16, 8
G = 4
N = B * S
E0, K0, CAP, I0 = 64, 6, 64, 88
SI = 2 * I0
E1, I1 = 8, 512
K1 = N * 2 // E1
NOWHERE = 2 * E0 * CAP
EPS = 1e-5
NEG = -1e9
FAR = -1e30
BLOCKS = 6
ROWS = BLOCKS * DK
QK = S + KV
UNROLL = 4
PAY0 = D + E0
PAY1 = D + E1


class Steps:

    def __init__(self, eng, sem, per_batch, b):
        self.eng, self.sem, self.per_batch, self.b, self.k = eng, sem, per_batch, b, 0

    def then(self, instruction, apart=False):
        self.k += 1
        instruction.then_inc(self.sem, 1)
        value = self.b * self.per_batch + self.k
        if apart:
            Apart.wait(self.eng, self.sem, value)
        else:
            self.eng.wait_ge(self.sem, value)

    def note(self, instruction):
        self.k += 1
        instruction.then_inc(self.sem, 1)

    def settle(self):
        self.eng.wait_ge(self.sem, self.b * self.per_batch + self.k)

    def end(self):
        assert self.k == self.per_batch, (self.k, self.per_batch)


class Apart:

    set_up = None

    @classmethod
    def wait(cls, eng, event, value):
        if not isinstance(value, int) or value > 0:
            if not isinstance(value, int):
                eng.lower_val(value)
            eng.wait_ge(cls.set_up, 1)
            eng.wait_ge(event, value)


class Named:
    pass


def pipelined(eng, step):
    def batches(i):
        return [b if 0 <= b < B else None for b in (i + 2, i + 1, i, i - 1, i - 2)]

    for i in range(-2, 4):
        step(*batches(i), i % 2)
    with eng.Fori(4, B - 3 - UNROLL, UNROLL) as i:
        for k in range(UNROLL):
            step(i + (k + 2), i + (k + 1), i + k, i + (k - 1), i + (k - 2), k % 2)
    for i in range(B - 4, B + 2):
        step(*batches(i), i % 2)




def at(tile, b):
    if isinstance(b, int):
        return tile[:, b, :]
    return tile[:, bass.ds(b, 1), :].rearrange("p o d -> p (o d)")


def row(dram, b):
    if isinstance(b, int):
        return dram[b]
    return dram[bass.ds(b, 1)].rearrange("o p d -> (o p) d")


def setup_block(nc, t, d, sem):
    loaded, consts, t.places_clear, gates, zero_made = (sem(x) for x in (
        "weights_loaded", "constants_step", "places_cleared", "gates_ready", "zeros_ready"))
    vstep, numbered, slots_made = sem("setup_vector_step"), sem("slots_numbered"), sem("slot_numbers_made")
    loads = [
        (t.wqT[0], d.wqT0), (t.wkT[0], d.wkT0), (t.wvT[0], d.wvT0), (t.woT[0], d.woT0),
        (t.wqT[1], d.wqT1), (t.wkT[1], d.wkT1), (t.wvT[1], d.wvT1), (t.woT[1], d.woT1),
        (t.gateT, d.gateT), (t.wrT, d.wrT), (t.ws13T, d.ws13T), (t.ws2T, d.ws2T),
        (t.qkvb, d.qkvb), (t.hs, d.hs),
        (t.outb, d.outb.partition_broadcast(128)), (t.gb, d.gb.partition_broadcast(128)),
        (t.graw, d.graw.partition_broadcast(128)),
        (t.mask_u8, d.mask0), (t.padT_u8, d.padT), (t.pad_u8, d.pad.partition_broadcast(128)),
    ]
    with nc.Block() as block:
        @block.sync
        def _(sp):
            for q in range(8):
                sp.dma_start(t.X[:, 4 * q:4 * q + 4, :],
                             d.x[4 * q:4 * q + 4].rearrange("b p d -> p b d")).then_inc(loaded, 16)
            for tile, src in loads:
                sp.dma_start(tile[:], src).then_inc(loaded, 16)
            sp.wait_ge(zero_made, 1)
            for q in range(4):
                sp.dma_start(d.places[q * 1024:(q + 1) * 1024, :].rearrange("(k p) w -> p k w", p=128),
                             t.zeros[:].rearrange("p (k w) -> p k w", w=PAY0)).then_inc(t.places_clear, 16)
            sp.sem_inc(Apart.set_up, 1)
            sp.wait_ge(loaded, 16 * (8 + len(loads)))

        @block.gpsimd
        def _(pool):
            c = Steps(pool, consts, 0, 0)
            select = lambda out, op, fill, base, pattern, cm: c.then(nc.gpsimd.affine_select(
                out=out, in_=out, compare_op=op, fill=fill, base=base, pattern=pattern, channel_multiplier=cm))
            nc.gpsimd.memset(t.zeros[:], 0.0).then_inc(zero_made, 1)
            nc.gpsimd.iota(t.iota_s[:], pattern=[[1, K1]], base=0, channel_multiplier=0).then_inc(numbered, 1)
            for tile in (t.ident, t.identb):
                c.then(nc.gpsimd.memset(tile[:], 0.0))
                select(tile[:], ALU.not_equal, 1.0, 0, [[-1, 128]], 1)
            c.then(nc.gpsimd.memset(t.before[:], 1.0))
            select(t.before[:], ALU.is_gt, 0.0, 0, [[1, 128]], -1)
            c.then(nc.gpsimd.memset(t.onesb[:], 1.0))
            c.then(nc.gpsimd.memset(t.pick[:], 0.0))
            for first in (0, 32):
                select(t.pick[:], ALU.not_equal, 1.0, -first, [[-1, H], [0, KV]], 1)
            c.then(nc.gpsimd.memset(t.headcols[:], 0.0))
            for i in range(G):
                c.then(nc.gpsimd.memset(t.headcols[:, i, i * DK:(i + 1) * DK], 1.0))
            c.then(nc.gpsimd.iota(t.iota_e[:], pattern=[[-CAP, E0]], base=NOWHERE, channel_multiplier=0))
            c.then(nc.gpsimd.tensor_copy(t.lastplace[:], t.iota_e[:]))
            c.then(nc.gpsimd.memset(t.minus_half[:], -0.5))
            for tile in (t.same, t.earlier):
                c.then(nc.gpsimd.memset(tile[:], 1.0))
                v = tile[:].rearrange("p (g r) -> p g r", g=4)
                select(v, ALU.is_ge, 0.0, 0, [[-32, 4], [0, 32]], 1)
                select(v, ALU.is_ge, 0.0, 31, [[32, 4], [0, 32]], -1)
            c.then(nc.gpsimd.tensor_copy(t.same_b[:], t.same[:]))
            select(t.earlier[:], ALU.is_gt, 0.0, 0, [[1, 128]], -1)
            c.then(nc.gpsimd.iota(t.iota_r[:], pattern=[[128, K1 // 128]], base=0, channel_multiplier=1))
            c.then(nc.gpsimd.tensor_copy(t.rank[:], t.iota_r[:]))
            c.then(nc.gpsimd.iota(t.iota_t[:], pattern=[[0, 1]], base=0, channel_multiplier=128))
            c.then(nc.gpsimd.tensor_copy(t.tile_start[:], t.iota_t[:]))
            for g in range(1, 4):
                c.then(nc.gpsimd.tensor_scalar(t.tile_start[32 * g:32 * g + 32, :], t.tile_start[32 * g:32 * g + 32, :],
                                               float(-N * g), None, ALU.add))
            for tile in (t.nmT, t.nm, t.sacc):
                c.then(nc.gpsimd.memset(tile[:], 0.0))

        @block.scalar
        def _(act):
            act.wait_ge(numbered, 1)
            nc.scalar.activation(t.slotno[:], t.iota_s[:], ACT.Copy).then_inc(slots_made, 1)
            act.wait_ge(loaded, 16 * (8 + len(loads)))
            nc.scalar.activation(t.gate[:], t.graw[:], ACT.Tanh).then_inc(gates, 1)

        @block.vector
        def _(dve):
            c = Steps(dve, vstep, 0, 0)
            for tile in (t.Qs, t.Ks, t.Vb):
                c.then(nc.vector.memset(tile[:], 0.0))
            dve.wait_ge(loaded, 16 * (8 + len(loads)))
            c.then(nc.vector.tensor_scalar(t.mask0[:], t.mask_u8[:], -NEG, NEG, ALU.mult, ALU.add))
            c.then(nc.vector.tensor_copy(t.mask_f[:], t.mask_u8[:]))
            c.then(nc.vector.tensor_reduce(t.rowany[:], t.mask_f[:], AX.X, ALU.max))
            c.then(nc.vector.tensor_scalar(t.padfar[:], t.pad_u8[:], FAR, None, ALU.mult))
            c.then(nc.vector.tensor_scalar(t.padinf[:], t.padT_u8[:], -3e38, 10.0, ALU.mult, ALU.mult))
            c.then(nc.vector.tensor_scalar(t.qbs[:], t.qkvb[:, 0:1], DK ** -0.5, None, ALU.mult))
            dve.wait_ge(gates, 1)
            c.then(nc.vector.tensor_scalar(t.outbg[:], t.outb[:], t.gate[:, 2:3], None, ALU.mult))


def attention_block(nc, L, t, d, sem_, ps):

    def sem(name):
        return sem_(f"{name}_{L}")

    ev = Named()
    ev.ctx_loaded = sem("ctx_loaded")
    ev.stored = sem("stored")
    ev.bounced = sem("bounced")
    ev.stats1 = sem("stats1")
    ev.rstd1 = sem("rstd1")
    ev.xn = sem("xn")
    ev.xT = sem("xT")
    ev.xTc = sem("xTc")
    ev.qkv = sem("qkv")
    ev.qf = sem("qf")
    ev.hi = sem("hi")
    ev.mid = sem("mid")
    ev.parts = sem("parts")
    ev.vb = sem("vb")
    ev.scores = sem("scores")
    ev.maxed = sem("maxed")
    ev.nm = sem("nm")
    ev.nmT = sem("nmT")
    ev.nmTc = sem("nmTc")
    ev.scoresT = sem("scoresT")
    ev.exped = sem("exped")
    ev.pv = sem("pv")
    ev.out = sem("out")
    ev.proj = sem("proj")
    ev.resid = sem("resid")
    ev.stats2 = sem("stats2")
    ev.rstd2 = sem("rstd2")
    ev.xn2 = sem("xn2")
    ev.xT2 = sem("xT2")
    ev.xT2c = sem("xT2c")
    ev.logits = sem("logits")
    ev.negmax = sem("negmax")
    ev.rexp = sem("rexp")
    ev.v0 = sem("v0")
    ev.v2 = sem("v2")
    ev.v3 = sem("v3")
    ev.v4 = sem("v4")
    ev.p1 = sem("p1")
    ev.p2 = sem("p2")
    ev.rest = sem("rest")
    if L == 0:
        ev.scattered = sem("scattered")
        ev.xkept = sem("xkept")
        ev.sel = sem("sel")
        ev.sacc = sem("sacc")
        ev.pos = sem("pos")
        ev.slot = sem("slot")
    else:
        ev.bias_loaded = sem("bias_loaded")
        ev.gathered = sem("gathered")
        ev.rows_stored = sem("rows_stored")
        ev.payload = sem("payload")
        ev.bias_parts = sem("bias_parts")
        ev.ysum = sem("ysum")
        ev.slots_fetched = sem("slots_fetched")
        ev.cleared = sem("cleared")
        ev.v1 = sem("v1")
    wq, wk, wv, wo = t.wqT[L], t.wkT[L], t.wvT[L], t.woT[L]
    M1, M2, PV, SM = ps[0], ps[1], ps[2], ps[3]
    SC, TA = ps[4:8], ps[6:8]
    xT_ps, qk_ps, v_ps = M1[:, 0:S], M1[:, S:S + QK], M1[0:KV, S + QK:S + QK + D]
    o_ps, xT2_ps, lg_ps = M2[:, 0:D], M2[:, 128:256], M2[:, 256:256 + (E0 if L == 0 else E1)]
    pos_ps = SC[0][:, 0:E0]
    nmT_ps = M1[0:48, 0:S // 2].bitcast(BF16)
    pv_ps, sum_ps = PV[:, 0:S], SM[:, 0:S]
    sc_w = E0 if L == 0 else E1
    attn_gate = t.gate[:, 2 * L:2 * L + 1]
    ffn_gate = t.gate[:, 1:2]

    def used(eng, event, value):
        if not isinstance(value, int) or value > 0:
            eng.wait_ge(event, value)

    with nc.Block() as block:
        @block.sync
        def _(sp):
            def load(n, u):
                Apart.wait(sp, ev.ctx_loaded, n * 16)
                used(sp, ev.qkv, n - 1)
                sp.dma_start(t.ctx[:, u, :], row(d.ctxT, n)).then_inc(ev.ctx_loaded, 16)
                if L == 1:
                    used(sp, ev.bias_loaded, n * 16)
                    used(sp, ev.bias_parts, n - 1)
                    sp.dma_start(t.fb[:, u, :], row(d.fside, n)).then_inc(ev.bias_loaded, 16)

            def bounce(n, u):
                qp, kp = t.parts[:, u, :, 0:S], t.parts[:, u, :, S:QK]
                q, k = d.scrq.rearrange("(b c) x -> c b x", c=D), d.scrk.rearrange("(b c) x -> c b x", c=D)

                def store(part, q_first, times, k_first):
                    sp.dma_start(q[:, q_first:q_first + times, :],
                                 qp[:, part:part + 1, :].broadcast_to([D, times, S])).then_inc(ev.stored, 16)
                    sp.dma_start(k[:, k_first:k_first + part + 1, :], kp[:, 0:part + 1, :]).then_inc(ev.stored, 16)

                Apart.wait(sp, ev.hi, n + 1)
                used(sp, ev.bounced, 32 * n)
                store(0, 0, 3, 5)
                Apart.wait(sp, ev.mid, n + 1)
                store(1, 3, 2, 3)
                Apart.wait(sp, ev.parts, n + 1)
                store(2, 5, 1, 0)
                Apart.wait(sp, ev.stored, 96 * (n + 1))
                used(sp, ev.scoresT, G * (n - 1))
                for stack, scr in ((t.Qs, d.scrq), (t.Ks, d.scrk)):
                    sp.dma_start(stack[0:ROWS, u, :, :].rearrange("p h x -> p (h x)"),
                                 scr.rearrange("(r h) x -> r (h x)", h=H)).then_inc(ev.bounced, 16)

            def store_rows(p, u):
                if L == 1:
                    Apart.wait(sp, ev.payload, p + 1)
                    used(sp, ev.rows_stored, 32 * p)
                    sp.dma_start(row(d.rows, p), t.payload[:, u, 0:PAY1]).then_inc(ev.rows_stored, 16)
                    sp.dma_start(row(d.out, p), at(t.X, p)).then_inc(ev.rows_stored, 16)

            def step(m, n, i, p, r, u):
                if m is not None:
                    load(m, u)
                if n is not None:
                    bounce(n, 1 - u)
                if r is not None:
                    store_rows(r, u)

            pipelined(sp, step)
            if L == 1:
                sp.wait_ge(ev.rows_stored, 32 * B)

        @block.tensor
        def _(pe):
            def transpose_x(n, u):
                pe.wait_ge(ev.xn, n + 1)
                used(pe, ev.vb, n)
                used(pe, ev.nmTc, n - 1)
                nc.tensor.transpose(xT_ps, t.xn[:, u, :], t.ident[:]).then_inc(ev.xT, 1)

            def project(n, u):
                pe.wait_ge(ev.xTc, n + 1)
                pe.wait_ge(ev.ctx_loaded, 16 * (n + 1))
                nc.tensor.matmul(qk_ps[:, 0:S], wq[:], t.xnT[:, u, :], start=True, stop=True)
                nc.tensor.matmul(qk_ps[:, S:QK], wk[:], t.ctx[:, u, :], start=True, stop=True)
                nc.tensor.matmul(v_ps, t.ctx[:, u, :], wv[:], start=True, stop=True).then_inc(ev.qkv, 1)

            def scores(i, u, g):
                if g == 0:
                    pe.wait_ge(ev.bounced, 32 * (i + 1))
                    if L == 1:
                        pe.wait_ge(ev.bias_parts, i + 1)
                used(pe, ev.maxed, G * i)
                if g == 2:
                    used(pe, ev.exped, G * i)
                if L == 0 and g == 0:
                    used(pe, ev.slot, i - 2)
                bank = SC[g][:, 0:G * KV].rearrange("p (j k) -> p j k", j=G)
                parts = [t.mask0[:]] if L == 0 else [t.bp[:, u, 0, :], t.bp[:, u, 1, :]]
                for k, part in enumerate(parts):
                    nc.tensor.matmul(bank, t.identb[:], part.unsqueeze(1).broadcast_to([S, G, KV]),
                                     start=(k == 0), stop=False)
                for j in range(G):
                    mm = nc.tensor.matmul(bank[:, j, :], t.Qs[:, u, G * j + g, :], t.Ks[:, u, G * j + g, :],
                                          start=False, stop=(j == G - 1))
                mm.then_inc(ev.scores, 1)

            def transpose_max(i, u):
                Apart.wait(pe, ev.nm, i + 1)
                if not isinstance(i, int) or i + 1 < B:
                    pe.wait_ge(ev.vb, i + 2)
                nc.tensor.transpose(nmT_ps, t.nm[:, u, :], t.identb[:]).then_inc(ev.nmT, 1)

            def scores_T(i, u, g):
                if g == 0:
                    pe.wait_ge(ev.nmTc, i + 1)
                if g >= 2:
                    pe.wait_ge(ev.exped, G * i + g - 1)
                bank = TA[g % 2][0:KV, :].rearrange("p (j q) -> p j q", j=G)
                parts = [t.mask0[:]] if L == 0 else [t.bp[:, u, k, :] for k in range(3)]
                for k, part in enumerate(parts):
                    nc.tensor.matmul(bank, part, t.identb[:].unsqueeze(1).broadcast_to([S, G, S]),
                                     start=(k == 0), stop=False)
                for j in range(G):
                    nc.tensor.matmul(bank[:, j, :], t.Ks[:, u, G * j + g, :], t.Qs[:, u, G * j + g, :],
                                     start=False, stop=False)
                    mm = nc.tensor.matmul(bank[:, j, :], t.pick[:, G * g + j, :], t.nmT[:, u, :],
                                          start=False, stop=(j == G - 1))
                mm.then_inc(ev.scoresT, 1)

            def values(i, u, g):
                pe.wait_ge(ev.exped, G * i + g + 1)
                if g == 0:
                    used(pe, ev.out, i)
                for out, col in ((pv_ps, None), (sum_ps, t.headcols)):
                    for j in range(G):
                        w = t.Vb[0:KV, u, j, 32 * g:32 * g + 32] if col is None else col[0:KV, g, :]
                        mm = nc.tensor.matmul(out[32 * j:32 * j + 32, :], w,
                                              t.PT[0:KV, g, S * j:S * j + S], start=(g == 0), stop=(g == G - 1))
                mm.then_inc(ev.pv, 1)

            def project_out(p, u):
                pe.wait_ge(ev.out, p + 1)
                used(pe, ev.rexp, p)
                nc.tensor.matmul(o_ps, t.oT[:, u, :], wo[:], start=True, stop=True).then_inc(ev.proj, 1)

            def transpose_x2(p, u):
                pe.wait_ge(ev.xn2, p + 1)
                nc.tensor.transpose(xT2_ps, t.payload[:, u, 0:D], t.ident[:]).then_inc(ev.xT2, 1)

            def logits(p, u):
                pe.wait_ge(ev.xkept if L == 0 else ev.xT2c, p + 1)
                w = t.gateT if L == 0 else t.wrT
                nc.tensor.matmul(lg_ps, t.xT2[:, u, :], w[:], start=True, stop=True).then_inc(ev.logits, 1)

            def positions(p, u):
                pe.wait_ge(ev.sel, p + 1)
                used(pe, ev.sacc, p)
                pe.wait_ge(ev.maxed, G * B if isinstance(p, int) and p + 2 >= B else G * (p + 2) + 1)
                nc.tensor.matmul(pos_ps, t.before[:], t.sel[:, u, :], start=True, stop=False)
                nc.tensor.matmul(pos_ps, t.onesb[:], t.sacc[:, u, :], start=False, stop=True).then_inc(ev.pos, 1)

            def step(m, n, i, p, r, u):
                if n is not None:
                    project(n, 1 - u)
                if i is not None:
                    scores(i, u, 2)
                    scores(i, u, 3)
                if p is not None:
                    project_out(p, 1 - u)
                if i is not None:
                    transpose_max(i, u)
                    scores_T(i, u, 0)
                    scores_T(i, u, 1)
                if r is not None and L == 0:
                    positions(r, u)
                if i is not None:
                    values(i, u, 0)
                    scores_T(i, u, 2)
                    values(i, u, 1)
                    scores_T(i, u, 3)
                if p is not None:
                    transpose_x2(p, 1 - u)
                if i is not None:
                    values(i, u, 2)
                if n is not None:
                    scores(n, 1 - u, 0)
                if m is not None:
                    transpose_x(m, u)
                if n is not None:
                    scores(n, 1 - u, 1)
                if i is not None:
                    values(i, u, 3)
                if p is not None:
                    logits(p, 1 - u)

            pipelined(pe, step)

        @block.scalar
        def _(act):
            def copy_projections(n, w):
                act.wait_ge(ev.qkv, n + 1)
                used(act, ev.parts, n - 1)
                used(act, ev.stored, 96 * (n - 1))
                qb, kb = (0.0, 0.0) if L == 0 else (t.qbs[:], t.qkvb[:, 1:2])
                nc.scalar.activation(t.qkf[:, w, 0:S], qk_ps[:, 0:S], ACT.Identity, bias=qb,
                                     scale=DK ** -0.5).then_inc(ev.qf, 1)
                nc.scalar.activation(t.qkf[:, w, S:QK], qk_ps[:, S:QK], ACT.Identity, bias=kb).then_inc(ev.qf, 1)
                used(act, ev.pv, G * (n - 1))
                nc.scalar.activation(
                    t.Vb[0:KV, w, :, :].rearrange("p j (i x) -> p j i x", x=40)[:, :, :, 0:DK],
                    v_ps.rearrange("p (j i d) -> p j i d", j=G, i=G), ACT.Copy).then_inc(ev.vb, 1)
                act.wait_ge(ev.qf, 2 * n + 2)
                nc.scalar.activation(t.parts[:, w, 0, :], t.qkf[:, w, :], ACT.Copy).then_inc(ev.hi, 1)

            def second_part(n, w):
                act.wait_ge(ev.rest, n + 1)
                nc.scalar.activation(t.parts[:, w, 1, :], t.rest[:], ACT.Copy).then_inc(ev.mid, 1)

            def copy_max(i, u):
                act.wait_ge(ev.nmT, i + 1)
                used(act, ev.scoresT, G * (i - 1))
                nc.scalar.activation(t.nmT[0:48, u, :], nmT_ps, ACT.Copy).then_inc(ev.nmTc, 1)

            def exponentials(i, g):
                Apart.wait(act, ev.scoresT, G * i + g + 1)
                Apart.wait(act, ev.pv, G * (i - 1) + g + 1)
                if L == 0:
                    pad = 0.0
                elif isinstance(i, int):
                    pad = t.padinf[0:KV, i:i + 1]
                else:
                    pad = t.padinf[0:KV, bass.ds(i, 1)]
                nc.scalar.activation(t.PT[0:KV, g, :], TA[g % 2][0:KV, :], ACT.Exp, bias=pad).then_inc(ev.exped, 1)

            def copy_x2(p, w):
                act.wait_ge(ev.xT2, p + 1)
                used(act, ev.logits, p - 1)
                nc.scalar.activation(t.xT2[:, w, :], xT2_ps, ACT.Copy).then_inc(ev.xT2c, 1)
                if L == 0:
                    nc.scalar.activation(at(t.XT, p), xT2_ps, ACT.Copy).then_inc(ev.xkept, 1)

            def copy_x(m, u):
                act.wait_ge(ev.xT, m + 1)
                used(act, ev.qkv, m - 1)
                nc.scalar.activation(t.xnT[:, u, :], xT_ps, ACT.Copy).then_inc(ev.xTc, 1)

            def router_exp(p, w):
                act.wait_ge(ev.negmax, p + 1)
                nc.scalar.activation(t.ex[:, w, 0:sc_w], lg_ps, ACT.Exp, bias=t.negmax[:, w, :],
                                     accum_out=t.exsum[:, w, :]).then_inc(ev.rexp, 1)

            def step(m, n, i, p, r, u):
                if n is not None:
                    copy_projections(n, 1 - u)
                if n is not None:
                    second_part(n, 1 - u)
                if i is not None:
                    copy_max(i, u)
                if i is not None:
                    for g in range(G):
                        exponentials(i, g)
                if p is not None:
                    copy_x2(p, 1 - u)
                if m is not None:
                    copy_x(m, u)
                if p is not None:
                    router_exp(p, 1 - u)

            pipelined(act, step)

        @block.gpsimd
        def _(pool):
            def rstd(b, u, k, stats, ready, stepsem):
                Apart.wait(pool, stats, b + 1)
                queries0 = L == 0 and k == 0
                c = Steps(pool, stepsem, 2 if queries0 else 1, b)
                c.then(nc.gpsimd.tensor_scalar(t.rs[:, k, u, :], t.mv[:, k, u, 1:2], EPS, None, ALU.add))
                power = nc.gpsimd.tensor_tensor(t.rstd[:, k, u, :], t.rs[:, k, u, :], t.minus_half[:], ALU.pow)
                if queries0:
                    c.then(power)
                    power = nc.gpsimd.tensor_tensor(t.rstd[:, k, u, :], t.rstd[:, k, u, :], t.rowany[:], ALU.mult)
                power.then_inc(ready, 1)
                c.end()

            def split(n, u):
                pool.wait_ge(ev.hi, n + 1)
                nc.gpsimd.tensor_tensor(t.rest[:], t.qkf[:, u, :], t.parts[:, u, 0, :],
                                        ALU.subtract).then_inc(ev.rest, 1)
                pool.wait_ge(ev.mid, n + 1)
                nc.gpsimd.tensor_tensor(t.parts[:, u, 2, :], t.rest[:], t.parts[:, u, 1, :],
                                        ALU.subtract).then_inc(ev.parts, 1)

            def clear(b, u):
                used(pool, ev.gathered, 16 * K0 * b)
                Apart.wait(pool, ev.ysum, b - 1)
                nc.gpsimd.tensor_copy(t.slotg[:, u, :], at(t.slots, b)).then_inc(ev.slots_fetched, 1)
                nc.gpsimd.memset(t.yrows[:, u, :, :], 0.0).then_inc(ev.cleared, 1)
                Apart.wait(pool, ev.slots_fetched, b + 1)
                Apart.wait(pool, ev.cleared, b + 1)

            def gather(b, u, choices):
                for j in choices:
                    nc.gpsimd.indirect_dma_start(
                        out=t.yrows[:, u, j, :], out_offset=None, in_=d.yplaces,
                        in_offset=bass.IndirectOffsetOnAxis(ap=t.slotg[:, u, j:j + 1], axis=0),
                        bounds_check=E0 * CAP - 1, oob_is_err=False).then_inc(ev.gathered, 16)

            def count(p, u):
                pool.wait_ge(ev.sel, p + 1)
                used(pool, ev.pos, p)
                used(pool, ev.sacc, p)
                nc.gpsimd.tensor_tensor(t.sacc[:, 1 - u, :], t.sacc[:, u, :], t.sel[:, u, :],
                                        ALU.add).then_inc(ev.sacc, 1)

            def scatter(p, u):
                pool.wait_ge(ev.slot, p + 1)
                Apart.wait(pool, ev.scattered, 16 * K0 * p)
                for j in range(K0):
                    nc.gpsimd.indirect_dma_start(
                        out=d.places, out_offset=bass.IndirectOffsetOnAxis(ap=t.slot[:, u, j:j + 1], axis=0),
                        in_=t.payload[:, u, 0:PAY0], in_offset=None,
                        bounds_check=E0 * CAP - 1, oob_is_err=False).then_inc(ev.scattered, 16)

            def step(m, n, i, p, r, u):
                if L == 1 and isinstance(m, int) and m == 0:
                    clear(0, 0)
                    gather(0, 0, range(K0))
                following = L == 1 and m is not None and not (isinstance(m, int) and m + 1 == B)
                if n is not None:
                    split(n, 1 - u)
                if p is not None:
                    rstd(p, 1 - u, 1, ev.stats2, ev.rstd2, ev.p2)
                if following:
                    clear(m + 1, 1 - u)
                    gather(m + 1, 1 - u, range(K0 // 2))
                if m is not None:
                    rstd(m, u, 0, ev.stats1, ev.rstd1, ev.p1)
                if following:
                    gather(m + 1, 1 - u, range(K0 // 2, K0))
                if L == 0 and r is not None:
                    count(r, u)
                    scatter(r, u)

            if L == 0:
                pool.wait_ge(t.places_clear, 64)
            pipelined(pool, step)
            if L == 0:
                pool.wait_ge(ev.scattered, 16 * K0 * B)

        @block.vector
        def _(dve):
            ve = nc.vector

            def stats(b, u, k, event, c):
                c.then(ve.bn_stats(t.st[:, k, :], at(t.X, b)), apart=True)
                ve.bn_aggr(t.mv[:, k, u, :], t.st[:, k, :]).then_inc(event, 1)

            def add_experts(n, u, c):
                dve.wait_ge(ev.gathered, 16 * K0 * (n + 1))
                ve.tensor_reduce(t.ysum[:], t.yrows[:, u, :, :].rearrange("p j d -> p d j"), AX.X,
                                 ALU.add).then_inc(ev.ysum, 1)
                dve.wait_ge(ev.ysum, n + 1)
                c.then(ve.scalar_tensor_tensor(at(t.X, n), t.ysum[:], ffn_gate, at(t.X, n), ALU.mult, ALU.add),
                       apart=True)

            def norm1(n, u, c):
                dve.wait_ge(ev.stats1, n + 1)
                dve.wait_ge(ev.rstd1, n + 1)
                used(dve, ev.xT, n - 1)
                ve.tensor_scalar(t.xn[:, u, :], at(t.X, n), t.mv[:, 0, u, 0:1], t.rstd[:, 0, u, :],
                                 ALU.subtract, ALU.mult).then_inc(ev.xn, 1)
                if L == 1:
                    dve.wait_ge(ev.xn, n + 1)
                    c.then(ve.tensor_tensor(at(t.X, n), at(t.X, n), t.outbg[:], ALU.add))

            def split_bias(n, u, c):
                dve.wait_ge(ev.bias_loaded, 16 * (n + 1))
                used(dve, ev.scoresT, G * (n - 1))
                c.then(ve.tensor_tensor(t.fb2[:, 0, :], t.fb[:, u, :], at(t.padfar_rows, n), ALU.add))
                c.then(ve.tensor_copy(t.bp[:, u, 0, :], t.fb2[:, 0, :]))
                c.then(ve.tensor_tensor(t.fb2[:, 1, :], t.fb2[:, 0, :], t.bp[:, u, 0, :], ALU.subtract))
                c.then(ve.tensor_copy(t.bp[:, u, 1, :], t.fb2[:, 1, :]))
                ve.tensor_tensor(t.bp[:, u, 2, :], t.fb2[:, 1, :], t.bp[:, u, 1, :],
                                 ALU.subtract).then_inc(ev.bias_parts, 1)

            def head_max(i, u, g):
                dve.wait_ge(ev.scores, G * i + g + 1)
                ve.tensor_reduce(t.mx[:, G * g:G * g + G],
                                 SC[g][:, 0:G * KV].rearrange("p (j k) -> p j k", j=G),
                                 AX.X, ALU.max).then_inc(ev.maxed, 1)

            def negate_max(i, u, c):
                dve.wait_ge(ev.maxed, G * (i + 1))
                used(dve, ev.nmT, i - 1)
                c.then(ve.tensor_scalar(t.nm[:, u, 0:H], t.mx[:], -1.0, None, ALU.mult))
                ve.scalar_tensor_tensor(t.nm[:, u, 32:32 + H], t.mx[:], -1.0, t.nm[:, u, 0:H], ALU.mult,
                                        ALU.subtract).then_inc(ev.nm, 1)
                dve.wait_ge(ev.nm, i + 1)

            def normalise(p, u, c):
                dve.wait_ge(ev.pv, G * (p + 1))
                c.then(ve.reciprocal(t.rsum[:], sum_ps))
                used(dve, ev.proj, p - 1)
                scaled = ve.tensor_tensor(t.oT[:, u, :], pv_ps, t.rsum[:], ALU.mult)
                if L == 1:
                    c.then(scaled)
                    scaled = ve.tensor_scalar(t.oT[:, u, :], t.oT[:, u, :], t.qkvb[:, 2:3], t.hs[:],
                                              ALU.add, ALU.mult)
                scaled.then_inc(ev.out, 1)

            def residual(p, u, c):
                dve.wait_ge(ev.proj, p + 1)
                ve.scalar_tensor_tensor(at(t.X, p), o_ps, attn_gate, at(t.X, p), ALU.mult,
                                        ALU.add).then_inc(ev.resid, 1)
                Apart.wait(dve, ev.resid, p + 1)
                stats(p, u, 1, ev.stats2, c)

            def norm2(p, u):
                dve.wait_ge(ev.stats2, p + 1)
                dve.wait_ge(ev.rstd2, p + 1)
                if L == 0:
                    used(dve, ev.scattered, 16 * K0 * (p - 1))
                    used(dve, ev.xT2, p - 1)
                else:
                    used(dve, ev.rows_stored, 32 * (p - 1))
                ve.tensor_scalar(t.payload[:, u, 0:D], at(t.X, p), t.mv[:, 1, u, 0:1], t.rstd[:, 1, u, :],
                                 ALU.subtract, ALU.mult).then_inc(ev.xn2, 1)

            def router_max(p, u, c):
                dve.wait_ge(ev.logits, p + 1)
                c.then(ve.tensor_reduce(t.lmax[:], lg_ps, AX.X, ALU.max))
                ve.tensor_scalar(t.negmax[:, u, :], t.lmax[:], -1.0, None, ALU.mult).then_inc(ev.negmax, 1)

            def router0(p, u, c):
                dve.wait_ge(ev.rexp, p + 1)
                c.then(ve.reciprocal(t.exrec[:], t.exsum[:, u, :]))
                c.note(ve.tensor_scalar(t.payload[:, u, D:PAY0], t.ex[:, u, :], t.exrec[:], None, ALU.mult))
                c.then(ve.scalar_tensor_tensor(t.biased[:], t.ex[:, u, :], t.exrec[:], t.gb[:], ALU.mult, ALU.add),
                       apart=True)
                c.then(ve.max(t.top8[:], t.biased[:]))
                c.note(ve.tensor_scalar(t.above[:], t.biased[:], t.top8[:, K0 - 1:K0], 0.0, ALU.is_gt, ALU.add,
                                        accum_out=t.n_above[:]))
                c.then(ve.tensor_scalar(t.equal[:], t.biased[:], t.top8[:, K0 - 1:K0], None, ALU.is_equal))
                c.note(ve.tensor_tensor_scan(t.n_equal[:], t.equal[:], t.equal[:], 0.0, ALU.add, ALU.max))
                c.then(ve.tensor_scalar(t.wanted[:], t.n_above[:], -1.0, float(K0), ALU.mult, ALU.add))
                c.then(ve.scalar_tensor_tensor(t.equal[:], t.n_equal[:], t.wanted[:], t.equal[:], ALU.is_le, ALU.mult))
                ve.tensor_tensor(t.sel[:, u, :], t.above[:], t.equal[:], ALU.add).then_inc(ev.sel, 1)
                dve.wait_ge(ev.sel, p + 1)

            def place(p, u, c):
                dve.wait_ge(ev.pos, p + 1)
                c.note(ve.scalar_tensor_tensor(t.fits[:], pos_ps, float(CAP), t.sel[:, u, :], ALU.is_lt, ALU.mult))
                c.then(ve.tensor_tensor(t.back[:], t.lastplace[:], pos_ps, ALU.subtract))
                c.then(ve.tensor_tensor(t.back[:], t.back[:], t.fits[:], ALU.mult), apart=True)
                c.then(ve.max(t.top8b[:], t.back[:]))
                c.then(ve.tensor_scalar(t.slot[:, u, :], t.top8b[:], -1.0, float(NOWHERE), ALU.mult, ALU.add))
                ve.tensor_copy(at(t.slots, p), t.slot[:, u, :]).then_inc(ev.slot, 1)

            def router1(p, u, c):
                dve.wait_ge(ev.rexp, p + 1)
                c.then(ve.reciprocal(t.exrec[:], t.exsum[:, u, :]))
                c.then(ve.tensor_scalar(t.payload[:, u, D:PAY1], t.ex[:, u, 0:E1], t.exrec[:], None, ALU.mult))
                dst = t.scores1[:, :, p:p + 1] if isinstance(p, int) else t.scores1[:, :, bass.ds(p, 1)]
                ve.tensor_copy(dst.rearrange("p e o -> p (e o)"), t.payload[:, u, D:PAY1]).then_inc(ev.payload, 1)

            def step(m, n, i, p, r, u):
                w = 1 - u
                s0 = None if m is None else Steps(dve, ev.v0, 1 if L == 0 else 3, m)
                s1 = None if n is None or L == 0 else Steps(dve, ev.v1, 4, n)
                s2 = None if i is None else Steps(dve, ev.v2, 1, i)
                s3 = None if p is None else Steps(dve, ev.v3, 3 if L == 0 else 4, p)
                s4 = None if r is None else Steps(dve, ev.v4, 14 if L == 0 else 2, r)
                if p is not None:
                    normalise(p, w, s3)
                if i is not None:
                    head_max(i, u, 2)
                    head_max(i, u, 3)
                    negate_max(i, u, s2)
                if r is not None:
                    (router0 if L == 0 else router1)(r, u, s4)
                if p is not None:
                    residual(p, w, s3)
                if m is not None:
                    if L == 1:
                        add_experts(m, u, s0)
                    stats(m, u, 0, ev.stats1, s0)
                if r is not None and L == 0:
                    place(r, u, s4)
                if n is not None and L == 1:
                    split_bias(n, w, s1)
                if p is not None:
                    norm2(p, w)
                if m is not None:
                    norm1(m, u, s0)
                if n is not None:
                    head_max(n, w, 0)
                    head_max(n, w, 1)
                if p is not None:
                    router_max(p, w, s3)
                for c in (s0, s1, s2, s3, s4):
                    if c is not None:
                        c.end()

            pipelined(dve, step)


def experts0_block(nc, t, d, sem, ps):
    T4 = 4
    NB = B // T4
    GE = 8
    NG = E0 // GE
    (s_h, s_e, s_u, s_z, s_zadd, r_w, r_w2, r_x, r_T, r_Tc, r_h, r_e, r_u, r_y, r_yo, r_wt, r_out) = (
        sem(f"mlp_{x}") for x in (
            "hidden", "silu", "gated", "out", "added",
            "weights_loaded", "out_weights_loaded", "places_loaded", "places_T", "places_T_copied", "expert_hidden",
            "expert_silu", "expert_gated", "expert_out", "expert_scaled", "scores_loaded", "rows_out"))
    H1 = ps[0], ps[2]
    H3 = ps[1], ps[3]
    Y = ps[4], ps[5]
    TP = ps[6]

    def later(eng, event, value):
        if not isinstance(value, int) or value > 0:
            eng.wait_ge(event, value)

    def groups(eng, body, last):
        body(0, 0)
        body(1, 1)
        body(2, 0)
        with eng.Fori(3, NG - 2, 2) as g:
            body(g, 1)
            body(g + 1, 0)
        body(NG - 1, 1)
        last(NG - 1, 1)

    with nc.Block() as block:
        @block.sync
        def _(sp):
            def load(g, u):
                Apart.wait(sp, r_w, 16 * g)
                later(sp, r_h, g - 1)
                cols = slice(GE * g, GE * g + GE) if isinstance(g, int) else bass.ds(g * GE, GE)
                sp.dma_start(t.w13[:, u, :, :], d.w13T[:, cols, :]).then_inc(r_w, 16)
                later(sp, r_x, 16 * g)
                later(sp, r_T, g - 1)
                pl = d.places.rearrange("(g k p) w -> g p k w", p=128, k=4)
                src = pl[g] if isinstance(g, int) else pl[bass.ds(g, 1)].rearrange("o p k w -> (o p) k w")
                sp.dma_start(t.xp[:, u, :, :], src[:, :, 0:D]).then_inc(r_x, 16)
                later(sp, r_w2, 16 * g)
                later(sp, r_y, g - 1)
                sp.dma_start(t.w2[:, u, :, :], d.w2T[:, cols, :]).then_inc(r_w2, 16)

            for half in range(2):
                src = bass.AP(tensor=d.places.tensor, offset=D + half * (CAP * PAY0 + 1),
                              ap=[[PAY0, CAP], [2 * (CAP * PAY0 + 1), E0 // 2]])
                sp.dma_start(t.wt[CAP * half:CAP * half + CAP, :], src,
                             allow_slow_non_contiguous=True).then_inc(r_wt, 16)
            groups(sp, load, lambda g, u: None)

        @block.gpsimd
        def _(pool):
            def store(g, u):
                Apart.wait(pool, r_yo, g + 1)
                Apart.wait(pool, r_out, 16 * g)
                pl = d.yplaces.rearrange("(g k p) w -> g p k w", p=128, k=4)
                dst = pl[g] if isinstance(g, int) else pl[bass.ds(g, 1)].rearrange("o p k w -> (o p) k w")
                pool.dma_start(dst, t.yo[:, u, :, :]).then_inc(r_out, 16)

            groups(pool, store, lambda g, u: None)
            pool.wait_ge(r_out, 16 * NG)

        @block.tensor
        def _(pe):
            def hidden(b, c):
                later(pe, s_u, 2 * b + c - 1)
                rhs = t.XT[:, T4 * b:T4 * b + T4, :] if isinstance(b, int) else t.XT[:, bass.ds(b * T4, T4), :]
                for k, bank in ((0, H1[c]), (1, H3[c])):
                    mm = nc.tensor.matmul(bank[0:I0, :], t.ws13T[:, (2 * k + c) * I0:(2 * k + c + 1) * I0],
                                          rhs.rearrange("p k q -> p (k q)"), start=True, stop=True)
                mm.then_inc(s_h, 1)

            def project(b):
                later(pe, s_zadd, b)
                pe.wait_ge(s_u, 2 * b + 2)
                for k in range(T4):
                    for c in range(2):
                        mm = nc.tensor.matmul(ps[4][:, D * k:D * k + D], t.uT[:, c, S * k:S * k + S],
                                              t.ws2T[:, c, :], start=(c == 0), stop=(c == 1))
                mm.then_inc(s_z, 1)

            hidden(0, 0)
            hidden(0, 1)

            def block4(b):
                hidden(b + 1, 0)
                project(b)
                hidden(b + 1, 1)

            block4(0)
            with pe.Fori(1, NB - 1) as b:
                block4(b)
            project(NB - 1)

            def places(g, u):
                pe.wait_ge(r_x, 16 * (g + 1))
                later(pe, r_Tc, g)
                for k in range(4):
                    mm = nc.tensor.transpose(TP[:, 128 * k:128 * k + 128], t.xp[:, u, k, :], t.ident[:])
                mm.then_inc(r_T, 1)

            def expert_hidden(g, u):
                pe.wait_ge(r_Tc, g + 1)
                pe.wait_ge(r_w, 16 * (g + 1))
                later(pe, r_u, g - 1)
                if isinstance(g, int) and g < 2:
                    pe.wait_ge(s_u, 2 * NB)
                for e in range(GE):
                    for k, bank in ((0, H1[u]), (1, H3[u])):
                        mm = nc.tensor.matmul(bank[0:I0, CAP * e:CAP * e + CAP], t.w13[:, u, e, k * I0:(k + 1) * I0],
                                              t.xpT[:, u, CAP * e:CAP * e + CAP], start=True, stop=True)
                mm.then_inc(r_h, 1)

            def outputs(g, u):
                pe.wait_ge(r_u, g + 1)
                pe.wait_ge(r_w2, 16 * (g + 1))
                later(pe, r_yo, g - 1)
                if isinstance(g, int) and g == 0:
                    pe.wait_ge(s_zadd, NB)
                for e in range(GE):
                    h = CAP * (e % 2)
                    mm = nc.tensor.matmul(Y[u][h:h + CAP, D * (e // 2):D * (e // 2) + D],
                                          t.gT[:, u, CAP * e:CAP * e + CAP], t.w2[:, u, e, :], start=True, stop=True)
                mm.then_inc(r_y, 1)

            def body(g, u):
                places(g, u)
                if not isinstance(g, int) or g >= 1:
                    outputs(g - 1, 1 - u)
                expert_hidden(g, u)

            groups(pe, body, outputs)

        @block.scalar
        def _(act):
            def block4(b):
                for c in range(2):
                    act.wait_ge(s_h, 2 * b + c + 1)
                    later(act, s_u, 2 * b + c - 1)
                    nc.scalar.activation(t.silu[:, c, :], H1[c][0:I0, :], ACT.Silu).then_inc(s_e, 1)

            block4(0)
            with act.Fori(1, NB) as b:
                block4(b)

            def body(g, u):
                act.wait_ge(r_T, g + 1)
                later(act, r_h, g - 1)
                nc.scalar.activation(t.xpT[:, u, :], TP[:, :], ACT.Copy).then_inc(r_Tc, 1)
                act.wait_ge(r_h, g + 1)
                later(act, r_u, g - 1)
                nc.scalar.activation(t.silu[:, u, :], H1[u][0:I0, :], ACT.Silu).then_inc(r_e, 1)

            act.wait_ge(s_u, 2 * NB)
            groups(act, body, lambda g, u: None)

        @block.vector
        def _(dve):
            def block4(b):
                for c in range(2):
                    dve.wait_ge(s_e, 2 * b + c + 1)
                    if c == 0:
                        later(dve, s_z, b)
                    nc.vector.tensor_tensor(t.uT[:, c, :], H3[c][0:I0, :], t.silu[:, c, :],
                                            ALU.mult).then_inc(s_u, 1)
                dve.wait_ge(s_z, b + 1)
                tiles = slice(0, T4) if isinstance(b, int) else bass.ds(b * T4, T4)
                rows = t.X[:, tiles, :].rearrange("p k d -> p (k d)")
                nc.vector.scalar_tensor_tensor(rows, ps[4][:, :], t.gate[:, 1:2], rows, ALU.mult,
                                               ALU.add).then_inc(s_zadd, 1)

            block4(0)
            with dve.Fori(1, NB) as b:
                block4(b)

            def scale(g, u):
                dve.wait_ge(r_y, g + 1)
                later(dve, r_out, 16 * (g - 1))
                w = t.wt[:, 4 * g:4 * g + 4] if isinstance(g, int) else t.wt[:, bass.ds(g * 4, 4)]
                nc.vector.tensor_tensor(t.yo[:, u, :, :], Y[u][:, :].rearrange("p (k d) -> p k d", k=4),
                                        w.unsqueeze(2).broadcast_to([128, 4, D]), ALU.mult).then_inc(r_yo, 1)

            def body(g, u):
                dve.wait_ge(r_e, g + 1)
                later(dve, r_y, g - 1)
                nc.vector.tensor_tensor(t.gT[:, u, :], H3[u][0:I0, :], t.silu[:, u, :], ALU.mult).then_inc(r_u, 1)
                if isinstance(g, int) and g == 0:
                    return
                scale(g - 1, 1 - u)

            dve.wait_ge(r_wt, 32)
            groups(dve, body, scale)


def choice_block(nc, t, d, sem, ps):
    turned, copied, vstep, summed, k_v, k_cnt, k_sum = (sem(f"choice_{x}") for x in (
        "scores_T", "scores_T_copied", "vector_step", "sums", "bit_step", "bit_counts", "bit_sums"))
    BIT_STEPS = 5
    BITS = 30
    with nc.Block() as block:
        @block.tensor
        def _(pe):
            for h in range(2):
                mm = nc.tensor.transpose(ps[0][:, 128 * h:128 * h + 128],
                                         t.scores1[:, 4 * h:4 * h + 4, :].rearrange("p e k -> p (e k)"), t.ident[:])
            mm.then_inc(turned, 1)
            with pe.Fori(0, BITS, BIT_STEPS) as k:
                for j in range(BIT_STEPS):
                    pe.wait_ge(k_cnt, 2 * (k + (j + 1)))
                    nc.tensor.matmul(ps[1][:, 0:2], t.same_b[:], t.cnt_b[:], start=True, stop=True).then_inc(k_sum, 1)
            for n, (weights, counts) in enumerate(((t.same, t.cnt), (t.earlier, t.cnt2), (t.earlier, t.cnt3))):
                pe.wait_ge(copied, n + 2)
                nc.tensor.matmul(ps[2 + n][:, 0:2], weights[:], counts[:], start=True, stop=True).then_inc(summed, 1)

        @block.vector
        def _(dve):
            ve = nc.vector
            c = Steps(dve, vstep, 0, 0)
            c.note(ve.memset(t.firsts[:], float(N)))
            c.note(ve.memset(t.lasts[:], 0.0))
            c.note(ve.tensor_copy(t.counts_hi[:, :, 128:129].rearrange("p e o -> p (e o)"),
                                  t.tile_start[:].broadcast_to([128, E1])))
            c.note(ve.memset(t.counts_lo[:, :, 128:129].rearrange("p e o -> p (e o)"), 0.0))
            dve.wait_ge(turned, 1)
            ve.tensor_copy(t.sT[:], ps[0][:, 0:256].rearrange("p (h q) -> p h q", h=2)).then_inc(copied, 1)
            dve.wait_ge(copied, 1)
            c.note(ve.memset(t.thr[:], 0))
            c.note(ve.memset(t.bitu[:], 0))
            c.then(ve.memset(t.bitf[:], float(2 ** (BITS - 1))))
            c.then(ve.tensor_copy(t.cand[:], t.bitf[:]))
            def find_bit(k):
                s = Steps(dve, k_v, 6, k)
                for h in range(2):
                    ve.tensor_scalar(t.junk[:, h, :], t.sT[:, h, :], t.cand[:, h:h + 1].bitcast(F32), 0.0,
                                     ALU.is_ge, ALU.add, accum_out=t.cnt_b[:, h:h + 1]).then_inc(k_cnt, 1)
                s.note(ve.tensor_tensor(t.thr[:], t.thr[:], t.bitu[:], ALU.bitwise_or))
                s.then(ve.tensor_scalar(t.nextu[:], t.bitf[:], 0.5, None, ALU.mult))
                s.then(ve.tensor_tensor(t.nextu[:], t.nextu[:], t.thr[:], ALU.bitwise_or))
                dve.wait_ge(k_sum, k + 1)
                s.then(ve.scalar_tensor_tensor(t.bitu[:], ps[1][:, 0:2], float(K1), t.bitf[:], ALU.is_ge, ALU.mult))
                s.note(ve.tensor_scalar(t.bitf[:], t.bitf[:], 0.5, None, ALU.mult))
                s.then(ve.tensor_tensor(t.cand[:], t.nextu[:], t.bitu[:], ALU.bitwise_or))

            with dve.Fori(0, BITS, BIT_STEPS) as first:
                for j in range(BIT_STEPS):
                    find_bit(first + j)
            c.then(ve.tensor_tensor(t.thr[:], t.thr[:], t.bitu[:], ALU.bitwise_or))
            for h in range(2):
                thr = t.thr[:, h:h + 1].bitcast(F32)
                c.note(ve.tensor_scalar(t.gt[:, h, :], t.sT[:, h, :], thr, 0.0, ALU.is_gt, ALU.add,
                                        accum_out=t.cnt[:, h:h + 1]))
                c.note(ve.tensor_scalar(t.eq[:, h, :], t.sT[:, h, :], thr, 0.0, ALU.is_equal, ALU.add,
                                        accum_out=t.cnt2[:, h:h + 1]))
            c.settle()
            ve.memset(t.junk[:, 0, 0:1], 0.0).then_inc(copied, 1)
            ve.memset(t.junk[:, 0, 1:2], 0.0).then_inc(copied, 1)
            for h in range(2):
                c.note(ve.tensor_tensor_scan(t.cum[:, h, :], t.eq[:, h, :], t.eq[:, h, :], 0.0, ALU.add, ALU.max))
            c.settle()
            dve.wait_ge(summed, 2)
            c.then(ve.tensor_scalar(t.left[:], ps[2][:, 0:2], -1.0, float(K1), ALU.mult, ALU.add))
            c.then(ve.tensor_tensor(t.left[:], t.left[:], ps[3][:, 0:2], ALU.subtract))
            for h in range(2):
                c.note(ve.scalar_tensor_tensor(t.eq[:, h, :], t.cum[:, h, :], t.left[:, h:h + 1], t.eq[:, h, :],
                                               ALU.is_le, ALU.mult))
            c.settle()
            c.then(ve.tensor_tensor(t.gt[:], t.gt[:], t.eq[:], ALU.add))
            for h in range(2):
                c.note(ve.tensor_tensor_scan(t.cum[:, h, :], t.gt[:, h, :], t.gt[:, h, :], 0.0, ALU.add, ALU.max))
            c.settle()
            c.then(ve.tensor_copy(t.cnt3[:], t.cum[:, :, 127:128].rearrange("p h o -> p (h o)")))
            ve.memset(t.junk[:, 0, 0:1], 0.0).then_inc(copied, 1)
            dve.wait_ge(summed, 3)
            c.note(ve.tensor_copy(t.first[:], ps[4][:, 0:2]))
            c.then(ve.tensor_tensor(t.last[:], ps[4][:, 0:2], t.cnt3[:], ALU.add))
            for e in range(E1):
                j, h = 32 * (e % 4), e // 4
                c.note(ve.tensor_copy(t.firsts[j:j + 32, e:e + 1], t.first[j:j + 32, h:h + 1]))
                c.note(ve.tensor_copy(t.lasts[j:j + 32, e:e + 1], t.last[j:j + 32, h:h + 1]))
                c.note(ve.tensor_scalar(t.counts_hi[:, e, 0:128], t.cum[:, h, :], t.first[:, h:h + 1], None, ALU.add))
            c.settle()
            for e in range(E1):
                c.note(ve.scalar_tensor_tensor(t.counts_lo[:, e, 0:128], t.cum[:, e // 4, :],
                                               t.first[:, e // 4:e // 4 + 1], t.counts_hi[:, e, 0:128],
                                               ALU.add, ALU.subtract))
            c.settle()


def experts1_block(nc, t, d, sem, ps):
    NT = K1 // 128
    C1 = I1 // 128
    ev = Named()
    ev.oh = sem("moe_oh")
    ev.counted = sem("moe_counted")
    ev.picked = sem("moe_picked")
    ev.listed = sem("moe_listed")
    ev.gathered = sem("moe_gathered")
    ev.turned = sem("moe_turned")
    ev.turned_copied = sem("moe_turned_copied")
    ev.hidden = sem("moe_hidden")
    ev.gelu = sem("moe_gelu")
    ev.out = sem("moe_out")
    ev.scaled = sem("moe_scaled")
    ev.added = sem("moe_added")
    ev.weights = sem("moe_weights")
    ev.v_range = sem("moe_v_range")
    ev.v_y = sem("moe_v_y")
    ev.gate_ready = sem("moe_gate_ready")
    ev.gather_list = sem("moe_gather_list")
    ev.add_list = sem("moe_add_list")
    HB, Y, TB = ps[0:4], ps[4:6], ps[6:8]

    def later(eng, event, value):
        if not isinstance(value, int) or value > 0:
            eng.wait_ge(event, value)

    def experts(eng, ahead, body):
        ahead(0, 0)
        body(0, 0)
        body(1, 1)
        with eng.Fori(2, E1 - 5, 2) as e:
            body(e, 0)
            body(e + 1, 1)
        for e in range(E1 - 4, E1):
            body(e, e % 2)

    def exists(e):
        return not isinstance(e, int) or e < E1

    with nc.Block() as block:
        @block.sync
        def _(sp):
            def load(e, u):
                Apart.wait(sp, ev.weights, 64 * e)
                later(sp, ev.scaled, 2 * (e - 1))
                sp.dma_start(t.w1x[:, u, :], row(d.w1x, e)).then_inc(ev.weights, 16)
                sp.dma_start(t.w2x[:, u, :, :].rearrange("p c d -> p (c d)"), row(d.w2x, e)).then_inc(ev.weights, 16)
                b1 = d.b1x[e] if isinstance(e, int) else d.b1x[bass.ds(e, 1)].rearrange("o p c -> (o p) c")
                sp.dma_start(t.b1x[:, u, :], b1).then_inc(ev.weights, 16)
                b2 = d.b2x[e:e + 1, :] if isinstance(e, int) else d.b2x[bass.ds(e, 1), :]
                sp.dma_start(t.b2x[:, u, :], b2.rearrange("o d -> (o d)").partition_broadcast(128)
                             ).then_inc(ev.weights, 16)

            def body(e, u):
                if exists(e + 1):
                    load(e + 1, 1 - u)

            experts(sp, load, body)

        @block.tensor
        def _(pe):
            def pick(e, k, copied=0):
                if k == 0:
                    pe.wait_ge(ev.oh, e + 1)
                later(pe, ev.counted, NT * e + k - 1)
                later(pe, ev.turned_copied, copied)
                nc.tensor.matmul(TB[k % 2][:, 0:129], t.oh[:, 128 * k:128 * k + 128], at(t.counts_hi, e),
                                 start=True, stop=False)
                nc.tensor.matmul(TB[k % 2][:, 0:129], t.oh[:, 128 * k:128 * k + 128], at(t.counts_lo, e),
                                 start=False, stop=True).then_inc(ev.picked, 1)

            def turn(e, u):
                pe.wait_ge(ev.gathered, 16 * NT * (e + 1))
                counted = NT * (e + 3)
                if isinstance(e, int):
                    counted = 2 * NT + NT // 2 if e == 0 else min(counted, NT * E1)
                pe.wait_ge(ev.counted, counted)
                for s in range(2):
                    for k in range(4):
                        mm = nc.tensor.transpose(TB[s][:, 128 * k:128 * k + 128], t.xg[:, u, 4 * s + k, 0:D],
                                                 t.ident[:])
                    mm.then_inc(ev.turned, 1)

            def hidden(e, u, s, picks=False):
                if s == 0:
                    pe.wait_ge(ev.weights, 64 * (e + 1))
                pe.wait_ge(ev.turned_copied, 2 * e + s + 1)
                for c in range(C1):
                    later(pe, ev.gelu, 8 * e + 4 * s + c - 3)
                    nc.tensor.matmul(HB[c][:, :], t.w1x[:, u, 128 * c:128 * c + 128],
                                     t.xgT[:, u, 512 * s:512 * s + 512], start=True, stop=True).then_inc(ev.hidden, 1)
                    if picks:
                        pick(2, NT // 2 + c, 2)

            def out(e, u, s):
                pe.wait_ge(ev.gelu, 8 * e + 4 * s + 4)
                later(pe, ev.scaled, 2 * e + s - 1)
                for k in range(4):
                    if s == 0 and exists(e + 3):
                        pick(e + 3, 2 * k, 2 * (e + 1) if k == 0 else 0)
                        pick(e + 3, 2 * k + 1, 2 * (e + 1) if k == 0 else 0)
                    for c in range(C1):
                        mm = nc.tensor.matmul(Y[s][:, D * k:D * k + D], t.ge[:, s, c, 128 * k:128 * k + 128],
                                              t.w2x[:, u, c, :], start=(c == 0), stop=(c == C1 - 1))
                    if k == 3:
                        mm.then_inc(ev.out, 1)

            def ahead(e, u):
                for q in (e, e + 1):
                    for k in range(NT):
                        pick(q, k)
                for k in range(NT // 2):
                    pick(2, k)
                turn(e, u)

            def body(e, u):
                hidden(e, u, 0, isinstance(e, int) and e == 0)
                hidden(e, u, 1)
                out(e, u, 0)
                if exists(e + 1):
                    turn(e + 1, 1 - u)
                out(e, u, 1)

            experts(pe, ahead, body)

        @block.scalar
        def _(act):
            def copy(e, u):
                for s in range(2):
                    act.wait_ge(ev.turned, 2 * e + s + 1)
                    later(act, ev.hidden, 8 * (e - 1))
                    nc.scalar.activation(t.xgT[:, u, 512 * s:512 * s + 512], TB[s][:, :],
                                         ACT.Copy).then_inc(ev.turned_copied, 1)

            def gelu(e, u, s):
                for c in range(C1):
                    act.wait_ge(ev.hidden, 8 * e + 4 * s + c + 1)
                    later(act, ev.out, 2 * e + s - 1)
                    nc.scalar.activation(t.ge[:, s, c, :], HB[c][:, :], ACT.Gelu,
                                         bias=t.b1x[:, u, c:c + 1]).then_inc(ev.gelu, 1)

            def body(e, u):
                gelu(e, u, 0)
                gelu(e, u, 1)
                if exists(e + 1):
                    copy(e + 1, 1 - u)

            experts(act, copy, body)

        @block.gpsimd
        def _(pool):
            def gather(e, u):
                pool.wait_ge(ev.listed, e + 1)
                later(pool, ev.gathered, 16 * NT * e)
                Apart.wait(pool, ev.turned, 2 * (e - 1))
                Apart.wait(pool, ev.gate_ready, e - 1)
                nc.gpsimd.tensor_copy(t.gather_token[:, u, :], at(t.tokens, e)).then_inc(ev.gather_list, 1)
                Apart.wait(pool, ev.gather_list, e + 1)
                for k in range(NT):
                    nc.gpsimd.indirect_dma_start(
                        out=t.xg[:, u, k, :], out_offset=None, in_=d.rows_flat,
                        in_offset=bass.IndirectOffsetOnAxis(ap=t.gather_token[:, u, k:k + 1], axis=0),
                        ).then_inc(ev.gathered, 16)

            def add(e, u):
                Apart.wait(pool, ev.added, 16 * NT * e)
                nc.gpsimd.tensor_copy(t.add_token[:, u, :], at(t.tokens, e)).then_inc(ev.add_list, 1)
                Apart.wait(pool, ev.add_list, e + 1)
                for k in range(NT):
                    if k % 4 == 0:
                        Apart.wait(pool, ev.scaled, 2 * e + k // 4 + 1)
                    nc.gpsimd.indirect_dma_start(
                        out=d.out_flat, out_offset=bass.IndirectOffsetOnAxis(ap=t.add_token[:, u, k:k + 1], axis=0),
                        in_=t.y1[:, u, k, :], in_offset=None, compute_op=ALU.add).then_inc(ev.added, 16)

            def ahead(e, u):
                gather(e, u)
                gather(e + 1, 1 - u)

            def body(e, u):
                if exists(e + 2):
                    gather(e + 2, u)
                add(e, u)

            experts(pool, ahead, body)
            pool.wait_ge(ev.added, 16 * NT * E1)

        @block.vector
        def _(dve):
            ve = nc.vector

            def ranges(e, u):
                s = Steps(dve, ev.v_range, 1, e)
                later(dve, ev.picked, NT * e)
                col = (lambda x: x[:, e:e + 1]) if isinstance(e, int) else (lambda x: x[:, bass.ds(e, 1)])
                s.then(ve.tensor_scalar(t.oh[:], t.slotno[:], col(t.firsts), None, ALU.is_ge))
                ve.scalar_tensor_tensor(t.oh[:], t.slotno[:], col(t.lasts), t.oh[:], ALU.is_lt,
                                        ALU.mult).then_inc(ev.oh, 1)

            def count(e, u, ks):
                for k in ks:
                    dve.wait_ge(ev.picked, NT * e + k + 1)
                    ve.tensor_scalar(t.junk2[:, k % 2, :], TB[k % 2][:, 0:128], t.rank[:, k:k + 1],
                                     TB[k % 2][:, 128:129], ALU.is_le, ALU.add,
                                     accum_out=t.tokf[:, u, k:k + 1]).then_inc(ev.counted, 1)

            def keep_list(e, u):
                dve.wait_ge(ev.counted, NT * (e + 1))
                ve.tensor_copy(at(t.tokens, e), t.tokf[:, u, :]).then_inc(ev.listed, 1)

            def gates(e, u):
                dve.wait_ge(ev.gathered, 16 * NT * (e + 1))
                col = slice(D + e, D + e + 1) if isinstance(e, int) else bass.ds(e + D, 1)
                ve.tensor_scalar(t.gs[:, u, :], t.xg[:, u, :, col].rearrange("p k o -> p (k o)"), t.gate[:, 3:4],
                                 None, ALU.mult).then_inc(ev.gate_ready, 1)
                dve.wait_ge(ev.gate_ready, e + 1)

            def scale(e, u, s):
                st = Steps(dve, ev.v_y, 2, e)
                st.k = s
                dve.wait_ge(ev.out, 2 * e + s + 1)
                later(dve, ev.added, 16 * NT * (e - 1))
                y = t.y1[:, u, 4 * s:4 * s + 4, :]
                st.then(ve.tensor_tensor(y, Y[s][:, :].rearrange("p (k d) -> p k d", k=4),
                                         t.b2x[:, u, :].unsqueeze(1).broadcast_to([128, 4, D]), ALU.add))
                ve.tensor_tensor(y, y, t.gs[:, u, 4 * s:4 * s + 4].unsqueeze(2).broadcast_to([128, 4, D]),
                                 ALU.mult).then_inc(ev.scaled, 1)

            def ahead(e, u):
                for q in (e, e + 1):
                    ranges(q, q)
                    count(q, q, range(NT))
                    keep_list(q, q)
                ranges(2, 0)
                count(2, 0, range(NT // 2))

            def body(e, u):
                if isinstance(e, int) and e == 0:
                    count(2, 0, range(NT // 2, NT))
                    keep_list(2, 0)
                gates(e, u)
                if exists(e + 3):
                    ranges(e + 3, 1 - u)
                    count(e + 3, 1 - u, range(NT))
                    keep_list(e + 3, 1 - u)
                scale(e, u, 0)
                scale(e, u, 1)

            experts(dve, ahead, body)


def flamingo_kernel(nc, **dram):
    d = Named()
    d.x = dram["x"]
    d.ctxT = dram["ctxT"]
    d.fside = dram["fside"]
    d.mask0 = dram["mask0"]
    d.pad = dram["pad"]
    d.padT = dram["padT"]
    d.graw = dram["graw"]
    d.wqT0 = dram["wqT0"]
    d.wkT0 = dram["wkT0"]
    d.wvT0 = dram["wvT0"]
    d.woT0 = dram["woT0"]
    d.wqT1 = dram["wqT1"]
    d.wkT1 = dram["wkT1"]
    d.wvT1 = dram["wvT1"]
    d.woT1 = dram["woT1"]
    d.qkvb = dram["qkvb"]
    d.outb = dram["outb"]
    d.hs = dram["hs"]
    d.gateT = dram["gateT"]
    d.gb = dram["gb"]
    d.wrT = dram["wrT"]
    d.ws13T = dram["ws13T"]
    d.ws2T = dram["ws2T"]
    d.w13T = dram["w13T"]
    d.w2T = dram["w2T"]
    d.w1x = dram["w1x"]
    d.w2x = dram["w2x"]
    d.b1x = dram["b1x"]
    d.b2x = dram["b2x"]
    d.out = dram["out"]
    d.scrq = nc.dram_tensor("query_stack", [BLOCKS * D, S], BF16, kind="Internal").ap()
    d.scrk = nc.dram_tensor("key_stack", [BLOCKS * D, KV], BF16, kind="Internal").ap()
    d.places = nc.dram_tensor("places", [E0 * CAP, PAY0], F32, kind="Internal").ap()
    d.yplaces = nc.dram_tensor("places_out", [E0 * CAP, D], F32, kind="Internal").ap()
    d.rows = nc.dram_tensor("token_rows", [B, S, PAY1], F32, kind="Internal").ap()
    d.rows_flat = d.rows.rearrange("b s w -> (b s) w")
    d.out_flat = d.out.rearrange("b s w -> (b s) w")

    with ExitStack() as ctx:
        def sem(name):
            return ctx.enter_context(nc.semaphore(name))

        t = Named()
        Apart.set_up = sem("set_up")

        def tile(where, name, shape, dt, partitions=128):
            return where.enter_context(nc.sbuf_tensor(name, [partitions] + shape, dt))

        t.X = tile(ctx, "X", [B, D], F32)
        t.gate = tile(ctx, "gate", [4], F32)
        t.graw = tile(ctx, "graw", [4], F32)
        t.ident = tile(ctx, "ident", [128], F32)
        t.identb = tile(ctx, "identb", [128], BF16)
        t.scores1 = tile(ctx, "scores1", [E1, B], F32)
        t.slots = tile(ctx, "slots", [B, 8], U32)
        t.minus_half = tile(ctx, "minus_half", [1], F32)
        t.XT = tile(ctx, "XT", [B, D], F32)
        t.tile_start = tile(ctx, "tile_start", [1], F32)
        t.rank = tile(ctx, "rank", [K1 // 128], F32)
        t.slotno = tile(ctx, "slotno", [K1], F32)
        t.same = tile(ctx, "same", [128], F32)
        t.same_b = tile(ctx, "same_b", [128], BF16)
        t.earlier = tile(ctx, "earlier", [128], F32)
        ps = [ctx.enter_context(nc.psum_tensor(f"bank{k}", [128, 512], F32)) for k in range(8)]
        with ExitStack() as ex0:
            t.ws13T = tile(ex0, "ws13T", [4 * I0], F32)
            t.gateT = tile(ex0, "gateT", [E0], F32)
            t.wrT = tile(ex0, "wrT", [E1], F32)
            t.silu = tile(ex0, "silu", [2, 512], F32, I0)
            t.uT = tile(ex0, "uT", [2, 512], F32, I0)
            t.gT = tile(ex0, "gT", [2, 512], F32, I0)
            t.ws2T = tile(ex0, "ws2T", [2, D], F32, I0)
            t.w13 = tile(ex0, "w13", [2, 8, 2 * I0], F32)
            t.w2 = tile(ex0, "w2", [2, 8, D], F32, I0)
            t.xp = tile(ex0, "xp", [2, 4, D], F32)
            t.xpT = tile(ex0, "xpT", [2, 512], F32)
            t.yo = tile(ex0, "yo", [2, 4, D], F32)
            t.wt = tile(ex0, "wt", [E0 // 2], F32)
            t.qkvb = tile(ex0, "qkvb", [3], F32)
            t.hs = tile(ex0, "hs", [1], F32)
            t.outb = tile(ex0, "outb", [D], F32)
            t.outbg = tile(ex0, "outbg", [D], F32)
            t.gb = tile(ex0, "gb", [E0], F32)
            t.mask_u8 = tile(ex0, "mask_u8", [KV], U8)
            t.mask_f = tile(ex0, "mask_f", [KV], F32)
            t.mask0 = tile(ex0, "mask0", [KV], BF16)
            t.rowany = tile(ex0, "rowany", [1], F32)
            t.pad_u8 = tile(ex0, "pad_u8", [B * KV], U8)
            t.padfar = tile(ex0, "padfar", [B * KV], F32)
            t.padT_u8 = tile(ex0, "padT_u8", [B], U8, KV)
            t.padinf = tile(ex0, "padinf", [B], F32, KV)
            t.qbs = tile(ex0, "qbs", [1], F32)
            t.zeros = tile(ex0, "zeros", [8 * PAY0], F32)
            t.before = tile(ex0, "before", [128], BF16)
            t.onesb = tile(ex0, "onesb", [128], BF16)
            t.pick = tile(ex0, "pick", [H, KV], BF16)
            t.iota_e = tile(ex0, "iota_e", [E0], I32)
            t.lastplace = tile(ex0, "lastplace", [E0], F32)
            t.iota_r = tile(ex0, "iota_r", [K1 // 128], I32)
            t.iota_s = tile(ex0, "iota_s", [K1], I32)
            t.iota_t = tile(ex0, "iota_t", [1], I32)
            t.ctx = tile(ex0, "ctx", [2, KV], F32)
            t.fb = tile(ex0, "fb", [2, KV], F32)
            t.fb2 = tile(ex0, "fb2", [2, KV], F32)
            t.bp = tile(ex0, "bp", [2, 3, KV], BF16)
            t.qkf = tile(ex0, "qkf", [2, QK], F32)
            t.parts = tile(ex0, "parts", [2, 3, QK], BF16)
            t.rest = tile(ex0, "rest", [QK], F32)
            t.Qs = tile(ex0, "Qs", [2, H, S], BF16)
            t.Ks = tile(ex0, "Ks", [2, H, KV], BF16)
            t.headcols = tile(ex0, "headcols", [G, 32], F32)
            t.Vb = tile(ex0, "Vb", [2, G, 160], F32)
            t.xn = tile(ex0, "xn", [2, D], F32)
            t.xnT = tile(ex0, "xnT", [2, D], F32)
            t.st = tile(ex0, "st", [2, 6], F32)
            t.mv = tile(ex0, "mv", [2, 2, 2], F32)
            t.rs = tile(ex0, "rs", [2, 2, 1], F32)
            t.rstd = tile(ex0, "rstd", [2, 2, 1], F32)
            t.mx = tile(ex0, "mx", [H], F32)
            t.nm = tile(ex0, "nm", [2, 48], BF16)
            t.nmT = tile(ex0, "nmT", [2, S], BF16)
            t.PT = tile(ex0, "PT", [G, 512], F32)
            t.rsum = tile(ex0, "rsum", [S], F32)
            t.oT = tile(ex0, "oT", [2, S], F32)
            t.payload = tile(ex0, "payload", [2, PAY0], F32)
            t.xT2 = tile(ex0, "xT2", [2, D], F32)
            t.lmax = tile(ex0, "lmax", [1], F32)
            t.negmax = tile(ex0, "negmax", [2, 1], F32)
            t.ex = tile(ex0, "ex", [2, E0], F32)
            t.exsum = tile(ex0, "exsum", [2, 1], F32)
            t.exrec = tile(ex0, "exrec", [1], F32)
            t.biased = tile(ex0, "biased", [E0], F32)
            t.top8 = tile(ex0, "top8", [8], F32)
            t.above = tile(ex0, "above", [E0], F32)
            t.n_above = tile(ex0, "n_above", [1], F32)
            t.equal = tile(ex0, "equal", [E0], F32)
            t.n_equal = tile(ex0, "n_equal", [E0], F32)
            t.wanted = tile(ex0, "wanted", [1], F32)
            t.sel = tile(ex0, "sel", [2, E0], BF16)
            t.sacc = tile(ex0, "sacc", [2, E0], BF16)
            t.fits = tile(ex0, "fits", [E0], F32)
            t.back = tile(ex0, "back", [E0], F32)
            t.top8b = tile(ex0, "top8b", [8], F32)
            t.slot = tile(ex0, "slot", [2, 8], U32)
            t.slotg = tile(ex0, "slotg", [2, 8], U32)
            t.yrows = tile(ex0, "yrows", [2, K0, D], F32)
            t.ysum = tile(ex0, "ysum", [D], F32)
            t.wqT = [tile(ex0, f"wqT{L}", [D], F32) for L in range(2)]
            t.wkT = [tile(ex0, f"wkT{L}", [D], F32) for L in range(2)]
            t.wvT = [tile(ex0, f"wvT{L}", [D], F32) for L in range(2)]
            t.woT = [tile(ex0, f"woT{L}", [D], F32) for L in range(2)]
            t.padfar_rows = t.padfar[:].rearrange("p (b k) -> p b k", b=B)
            setup_block(nc, t, d, sem)
            attention_block(nc, 0, t, d, sem, ps)
            experts0_block(nc, t, d, sem, ps)
            attention_block(nc, 1, t, d, sem, ps)
        with ExitStack() as ex1:
            t.sT = tile(ex1, "sT", [2, 128], F32)
            t.thr = tile(ex1, "thr", [2], U32)
            t.bitf = tile(ex1, "bitf", [2], F32)
            t.bitu = tile(ex1, "bitu", [2], U32)
            t.nextu = tile(ex1, "nextu", [2], U32)
            t.cnt_b = tile(ex1, "cnt_b", [2], BF16)
            t.cand = tile(ex1, "cand", [2], U32)
            t.junk = tile(ex1, "junk", [2, 128], F32)
            t.cnt = tile(ex1, "cnt", [2], F32)
            t.cnt2 = tile(ex1, "cnt2", [2], F32)
            t.cnt3 = tile(ex1, "cnt3", [2], F32)
            t.gt = tile(ex1, "gt", [2, 128], F32)
            t.eq = tile(ex1, "eq", [2, 128], F32)
            t.cum = tile(ex1, "cum", [2, 128], F32)
            t.left = tile(ex1, "left", [2], F32)
            t.first = tile(ex1, "first", [2], F32)
            t.last = tile(ex1, "last", [2], F32)
            t.firsts = tile(ex1, "firsts", [E1], F32)
            t.lasts = tile(ex1, "lasts", [E1], F32)
            t.counts_hi = tile(ex1, "counts_hi", [E1, 129], BF16)
            t.counts_lo = tile(ex1, "counts_lo", [E1, 129], BF16)
            t.oh = tile(ex1, "oh", [K1], BF16)
            t.junk2 = tile(ex1, "junk2", [2, 128], F32)
            t.tokf = tile(ex1, "tokf", [2, 8], F32)
            t.tokens = tile(ex1, "tokens", [E1, K1 // 128], U32)
            t.gather_token = tile(ex1, "gather_token", [2, K1 // 128], U32)
            t.add_token = tile(ex1, "add_token", [2, K1 // 128], U32)
            t.xg = tile(ex1, "xg", [2, 8, PAY1], F32)
            t.xgT = tile(ex1, "xgT", [2, K1], F32)
            t.ge = tile(ex1, "ge", [2, 4, 512], F32)
            t.y1 = tile(ex1, "y1", [2, 8, D], F32)
            t.gs = tile(ex1, "gs", [2, 8], F32)
            t.w1x = tile(ex1, "w1x", [2, I1], F32)
            t.w2x = tile(ex1, "w2x", [2, 4, D], F32)
            t.b1x = tile(ex1, "b1x", [2, 4], F32)
            t.b2x = tile(ex1, "b2x", [2, D], F32)
            choice_block(nc, t, d, sem, ps)
            experts1_block(nc, t, d, sem, ps)




def laid_out(i):
    import numpy as np

    def head_last(w):
        return w.reshape(w.shape[0], H, DK).transpose(0, 2, 1).reshape(w.shape[0], D)

    inw, inb = i["L1_xattn_in_proj_weight"], i["L1_xattn_in_proj_bias"]
    qb, kb, vb = inb.reshape(3, D)
    perm = lambda v: v.reshape(H, DK).T.reshape(D)
    a = {
        "x": i["x"],
        "ctxT": i["ctx_1024"].transpose(0, 2, 1),
        "fside": i["fside_BxSxS2_0"],
        "mask0": i["mask_1x1xSxS2_bk0"].reshape(S, KV),
        "pad": i["mask_BxS2_bf0"].reshape(B * KV),
        "padT": np.ascontiguousarray(i["mask_BxS2_bf0"].T),
        "graw": np.stack([i["g_xattn"][0], i["g_ffn"][0], i["g_xattn"][1], i["g_ffn"][1]]),
        "wqT0": head_last(i["L0_xattn_w_q"].T), "wkT0": head_last(i["L0_xattn_w_k"].T),
        "wvT0": i["L0_xattn_w_v"].T, "woT0": i["L0_xattn_w_o"].T,
        "wqT1": head_last(inw[0:D].T), "wkT1": head_last(inw[D:2 * D].T),
        "wvT1": inw[2 * D:].T, "woT1": i["L1_xattn_out_w"].T,
        "qkvb": np.stack([perm(qb), perm(kb), vb], axis=1), "outb": i["L1_xattn_out_b"],
        "hs": np.repeat(i["L1_xattn_head_scales"], DK)[:, None],
        "gateT": i["L0_ffn_gate_w"].T, "gb": i["L0_ffn_gate_b"], "wrT": i["L1_ffn_Wr"],
        "ws13T": np.concatenate([i["L0_ffn_ws1"].T, i["L0_ffn_ws3"].T], axis=1),
        "ws2T": i["L0_ffn_ws2"].T.reshape(2, I0, D).transpose(1, 0, 2),
        "w13T": np.concatenate([i["L0_ffn_w1"], i["L0_ffn_w3"]], axis=1).transpose(2, 0, 1),
        "w2T": i["L0_ffn_w2"].transpose(2, 0, 1),
        "w1x": i["L1_ffn_W1"],
        "w2x": i["L1_ffn_W2"].reshape(E1, 4, 128, D).transpose(0, 2, 1, 3).reshape(E1, 128, 4 * D),
        "b1x": i["L1_ffn_b1"].reshape(E1, 4, 128).transpose(0, 2, 1), "b2x": i["L1_ffn_b2"],
    }
    return {k: np.ascontiguousarray(v) for k, v in a.items()}


def kernel(**inputs):
    import numpy as _np
    import concourse.bacc as _bacc
    from concourse import mybir as _mybir
    from concourse.bass_utils import run_bass_kernel_spmd as _run

    nc = _bacc.Bacc("TRN2", target_bir_lowering=False, num_devices=1)
    arrays = laid_out({k: _np.asarray(v) for k, v in inputs.items()})
    args = {k: nc.dram_tensor(f"in_{k}", a.shape, _mybir.dt.from_np(a.dtype), kind="ExternalInput").ap()
            for k, a in arrays.items()}
    args["out"] = nc.dram_tensor("out_0", (B, S, D), _mybir.dt.float32, kind="ExternalOutput").ap()
    flamingo_kernel(nc, **args)
    r = _run(nc, [{f"in_{k}": a for k, a in arrays.items()}], core_ids=[0])
    return r.results[0]["out_0"]
```
